# Optimizing a Trainium2 kernel written in Bass

```python
import numpy as np
import jax
import jax.numpy as jnp

def _softmax(x, axis=-1):
    return jax.nn.softmax(x, axis=axis)

def _gelu(x):
    return jax.nn.gelu(x, approximate=True)

def _silu(x):
    return jax.nn.silu(x)

def _sigmoid(x):
    return jax.nn.sigmoid(x)

def _layernorm(x, axis=-1, eps=1e-05):
    m = jnp.mean(x, axis=axis, keepdims=True)
    v = jnp.var(x, axis=axis, keepdims=True)
    return (x - m) / jnp.sqrt(v + eps)

def _scatter_add(tgt, idx, src, axis=0):
    return tgt.at[idx].add(src)

def _segment_sum(src, seg, n):
    return jax.ops.segment_sum(src, seg, n)
kernel_name = 'mk_gnn_preln_d1_gnn_r8_870089'

def setup_inputs(seed: int=0):
    np.random.seed(seed)
    _w = jnp.asarray

    def _rec_inputs():
        import jax
        import jax.numpy as jnp
        _gk = jax.random.key(seed)
        x = -0.000202 + 1 * jax.random.normal(jax.random.fold_in(_gk, 1), (6250, 128), jnp.float32)
        src = jax.random.randint(jax.random.fold_in(_gk, 2), (200000,), 0, 6250, jnp.int32)
        dst = jnp.minimum((6250 * jax.random.uniform(jax.random.fold_in(_gk, 3), (200000,)) ** 2.0).astype(jnp.int32), 49999)
        _o = jnp.argsort(dst, stable=True)
        src = src[_o]
        dst = dst[_o]
        edge_type_30 = jax.random.randint(jax.random.fold_in(_gk, 12), (200000,), 0, 30, jnp.int32)
        return (x, src, dst, edge_type_30)
    x, src, dst, edge_type_30 = _rec_inputs()

    def _L0_gnn_setup():
        import jax, jax.numpy as jnp
        import numpy as np
        N_NODES = 6250
        N_EDGES = 75000
        D_IN = 128
        D_OUT = 128
        NUM_REL = 10
        key = jax.random.key(seed)
        k_x, k_ei, k_et, k_w, k_b = jax.random.split(key, 5)
        x = jax.random.normal(k_x, (N_NODES, D_IN), dtype=jnp.float32)
        edge_index = jax.random.randint(k_ei, (2, N_EDGES), 0, N_NODES, dtype=jnp.int64)
        edge_types = jax.random.randint(k_et, (N_EDGES,), 0, 3 * NUM_REL, dtype=jnp.int64)
        bound = 1.0 / np.sqrt(D_IN)
        W = jax.random.uniform(k_w, (3, D_IN, D_OUT), minval=-bound, maxval=bound, dtype=jnp.float32)
        b = jax.random.uniform(k_b, (3, D_OUT), minval=-bound, maxval=bound, dtype=jnp.float32)
        return {'x': x, 'edge_index': edge_index, 'edge_types': edge_types, 'W': W, 'b': b}
    _L0_gnn_all = _L0_gnn_setup()
    _L0_gnn_in = {k: v for k, v in _L0_gnn_all.items() if k in ('W', 'b')}
    del _L0_gnn_all
    return {'x': x, 'src': src, 'dst': dst, 'edge_type_30': edge_type_30, 'L0_gnn_W': _L0_gnn_in['W'], 'L0_gnn_b': _L0_gnn_in['b']}

def reference(x, src, dst, edge_type_30, L0_gnn_W, L0_gnn_b):
    import jax
    import jax.numpy as jnp

    def _L0_gnn_ref(x, edge_index, edge_types, W, b):
        import jax, jax.numpy as jnp
        import numpy as np
        N_NODES = 6250
        N_EDGES = 75000
        D_IN = 128
        D_OUT = 128
        NUM_REL = 10
        src, dst = (edge_index[0], edge_index[1])
        src_feat = x[src]
        group = jnp.clip(edge_types // NUM_REL, 0, 2)
        msg = jnp.zeros((src_feat.shape[0], D_OUT), dtype=x.dtype)
        for g in range(3):
            mask = (group == g).astype(x.dtype)[:, None]
            msg = msg + mask * (src_feat @ W[g] + b[g])
        out = jax.ops.segment_sum(msg, dst, num_segments=x.shape[0])
        deg = jax.ops.segment_sum(jnp.ones_like(dst, dtype=x.dtype), dst, num_segments=x.shape[0])
        deg = jnp.maximum(deg, 1.0)
        return jax.nn.relu(out / deg[:, None])
    edge_index = jnp.stack([src, dst])
    h = jnp.maximum(_layernorm(x, axis=-1), 0.0)
    x = x + _L0_gnn_ref(h, edge_index, edge_type_30, L0_gnn_W, L0_gnn_b)
    return x

_drawn_inputs = setup_inputs


def setup_inputs(seed=0):
    import zlib

    import numpy as np

    out = dict(_drawn_inputs(seed))
    spreads = {}
    factors = {'L0_gnn_b': 3.052}
    for name, (base, spread) in spreads.items():
        noise = np.random.default_rng([zlib.crc32(name.encode()), seed]).standard_normal(out[name].shape)
        drawn = base * np.exp(spread * noise) if base else spread * noise
        out[name] = jnp.asarray(drawn.astype(out[name].dtype))
    for name, factor in factors.items():
        out[name] = (out[name] * factor).astype(out[name].dtype)
    return out
```

```python
from contextlib import ExitStack

import concourse.bass as bass
from concourse import mybir

F32 = mybir.dt.float32
BF16 = mybir.dt.bfloat16
I32 = mybir.dt.int32
ALU = mybir.AluOpType
ACT = mybir.ActivationFunctionType
AX_X = mybir.AxisListType.X

P = 128
GROUP = 8
RING = 5
REL_EDGE = 10
EPS = 1e-5
YBUF = 4


def bass_gnn_mean_aggregate_kernel(
    nc: bass.Bass,
    x: bass.AP,
    src: bass.AP,
    dst: bass.AP,
    edge_type: bass.AP,
    W: bass.AP,
    b: bass.AP,
    out: bass.AP,
):
    N, D = x.shape
    E = src.shape[0]
    R = W.shape[0]
    RD = R * D
    BLOCKS = -(-N // P)
    NPAD = BLOCKS * P
    LAST_ROWS = N - (BLOCKS - 1) * P
    TILES = -(-E // P)
    LAST_EDGES = E - (TILES - 1) * P
    GROUPS = TILES // GROUP
    TAIL = TILES - GROUPS * GROUP
    assert GROUPS % RING == 0 and 0 < TAIL < GROUP and D == P
    SLABS = -(-TILES // P)
    FULL_SLABS = TILES // P
    REST_TILES = TILES - FULL_SLABS * P - 1
    DA = D + 1
    TPP = 4
    XCH = 7
    SLABS_E = -(-SLABS // TPP)
    assert BLOCKS % XCH == 0
    CH = BLOCKS // XCH

    table = nc.dram_tensor("node_table", (R * NPAD, D), F32, kind="Internal").ap()

    with ExitStack() as ctx:
        def sb(name, shape, dt):
            return ctx.enter_context(nc.sbuf_tensor(name, shape, dt))

        def ps(name, shape, dt=F32):
            return ctx.enter_context(nc.psum_tensor(name, shape, dt))

        def sem(name):
            return ctx.enter_context(nc.semaphore(name))

        x_sb = sb("x_sb", [P, BLOCKS, D], F32)
        stats = sb("stats", [P, XCH, 6], F32)
        mv = sb("mv", [P, BLOCKS, 2], F32)
        var_eps = sb("var_eps", [P, BLOCKS], F32)
        std = sb("std", [P, BLOCKS], F32)
        rstd = sb("rstd", [P, BLOCKS], F32)
        normed = sb("normed", [P, 4, D], F32)
        hT = sb("hT", [P, 2, P], F32)
        y_sb = sb("y_sb", [P, YBUF, RD], F32)
        w_sb = sb("w_sb", [P, R, D], F32)
        b3 = sb("b3", [3, RD], F32)
        b_rest = sb("b_rest", [3, RD], F32)
        b_part = sb("b_part", [3, 3, RD], BF16)
        b_sum = sb("b_sum", [3, RD], F32)
        b_split = sb("b_split", [3, RD], BF16)
        ones3 = sb("ones3", [3, P], BF16)
        ident = sb("ident", [P, P], F32)
        src_rows = sb("src_rows", [P, SLABS, P], I32)
        dst_rows = sb("dst_rows", [P, SLABS, P], I32)
        type_rows = sb("type_rows", [P, SLABS, P], I32)
        row_rows = sb("row_rows", [P, SLABS, P], I32)
        rowf_rows = sb("rowf_rows", [P, SLABS, P], F32)
        shift_rows = sb("shift_rows", [P, SLABS, P], I32)
        dstf_rows = sb("dstf_rows", [P, SLABS, P], F32)
        row_idx = sb("row_idx", [P, SLABS * P], I32)
        idx_ring = sb("idx_ring", [P, RING, GROUP], I32)
        dst_col = sb("dst_col", [P, SLABS * P], F32)
        tile_min = sb("tile_min", [P, SLABS], F32)
        tile_max = sb("tile_max", [P, SLABS], F32)
        NG = GROUPS + 1
        edge_ends = sb("edge_ends", [1, 2, NG], F32)
        ends_int = sb("ends_int", [1, 2, NG], I32)
        win_ends = sb("win_ends", [1, 2, NG], I32)
        win_count = sb("win_count", [1, NG], F32)
        win_upto = sb("win_upto", [1, NG], F32)
        zeros1 = sb("zeros1", [1, NG], F32)
        plan = sb("plan", [1, NG, 3], I32)
        iota = sb("iota", [P, NPAD], F32)
        onehot = sb("onehot", [P, GROUP, P], F32)
        msg = sb("msg", [P, RING, GROUP, DA], F32)
        sums = sb("sums", [P, BLOCKS, DA], F32)
        deg = sb("deg", [P, BLOCKS], F32)
        rdeg = sb("rdeg", [P, BLOCKS], F32)
        mean = sb("mean", [P, XCH, D], F32)

        ps_t = [ps(f"ps_t{i}", [P, P]) for i in range(2)]
        ps_y = [ps(f"ps_y{i}", [P, RD]) for i in range(2)]
        ps_e = [ps(f"ps_e{i}", [P, TPP * P]) for i in range(2)]
        ps_sum = ps("ps_sum", [P, DA])

        x_landed = [sem(f"x_landed{c}") for c in range(CH)]
        pads_set = sem("pads_set")
        edges_landed = sem("edges_landed")
        consts_landed = sem("consts_landed")
        ident_made = sem("ident_made")
        iota_made = sem("iota_made")
        rows_made = sem("rows_made")
        b_steps = sem("b_steps")
        ends_made = sem("ends_made")
        stats_made = sem("stats_made")
        var_made = sem("var_made")
        std_made = sem("std_made")
        rstd_made = sem("rstd_made")
        centred = sem("centred")
        turned = sem("turned")
        relu_made = sem("relu_made")
        projected = sem("projected")
        y_copied = sem("y_copied")
        y_stored = [sem(f"y_stored{i}") for i in range(YBUF)]
        edges_turned = sem("edges_turned")
        edges_copied = sem("edges_copied")
        ends_turned = sem("ends_turned")
        plan_steps = sem("plan_steps")
        plan_made = sem("plan_made")
        ones_set = sem("ones_set")
        sums_zeroed = sem("sums_zeroed")
        gathered = [sem(f"gathered{i}") for i in range(RING)]
        tail_gathered = sem("tail_gathered")
        groups_begun = sem("groups_begun")
        idx_copied = sem("idx_copied")
        slots_free = sem("slots_free")
        onehot_made = sem("onehot_made")
        window_summed = sem("window_summed")
        window_added = sem("window_added")
        rdeg_made = sem("rdeg_made")
        mean_made = sem("mean_made")
        result_made = sem("result_made")
        result_stored = sem("result_stored")

        block = ctx.enter_context(nc.Block())

        x_blocks = x[0:(BLOCKS - 1) * P, :].rearrange("(w p) f -> p w f", p=P)
        out_blocks = out[0:(BLOCKS - 1) * P, :].rearrange("(w p) f -> p w f", p=P)
        table_rows = table.rearrange("(g w p) f -> w p g f", g=R, p=P)
        PADS = 4

        def edge_loads(eng, sb_rows, dram, twice):
            eng.dma_start(sb_rows[:, 0:FULL_SLABS, :],
                          dram[0:FULL_SLABS * P * P].rearrange("(s p e) -> p s e", p=P, e=P)).then_inc(edges_landed, 16)
            rest = FULL_SLABS * P * P
            eng.dma_start(sb_rows[0:REST_TILES, FULL_SLABS, :],
                          dram[rest:rest + REST_TILES * P].rearrange("(p e) -> p e", e=P)).then_inc(edges_landed, 16)
            last = dram[E - LAST_EDGES:E].rearrange("(a e) -> a e", a=1)
            eng.dma_start(sb_rows[REST_TILES:REST_TILES + 1, FULL_SLABS, 0:LAST_EDGES], last).then_inc(edges_landed, 16)
            if twice:
                eng.dma_start(sb_rows[REST_TILES:REST_TILES + 1, FULL_SLABS, LAST_EDGES:2 * LAST_EDGES],
                              last).then_inc(edges_landed, 16)
        assert 2 * LAST_EDGES == P
        EDGE_DMAS = 10

        @block.sync
        def _(sp):
            sp.wait_ge(pads_set, PADS)
            edge_loads(sp, dst_rows, dst, True)
            edge_loads(sp, src_rows, src, False)
            edge_loads(sp, type_rows, edge_type, False)
            for w in range(BLOCKS):
                sp.wait_ge(y_copied, w + 1)
                sp.dma_start(table_rows[w], y_sb[:, w % YBUF, :].rearrange("p (g f) -> p g f", g=R)).then_inc(
                    y_stored[w % YBUF], 16)
            for c in range(CH):
                sp.wait_ge(result_made, c + 1)
                w0, w1 = c * XCH, (c + 1) * XCH
                if c < CH - 1:
                    sp.dma_start(out_blocks[:, w0:w1, :], x_sb[:, w0:w1, :]).then_inc(result_stored, 16)
                else:
                    sp.dma_start(out_blocks[:, w0:w1 - 1, :], x_sb[:, w0:w1 - 1, :]).then_inc(result_stored, 16)
                    sp.dma_start(out[N - LAST_ROWS:N, :], x_sb[0:LAST_ROWS, w1 - 1, :]).then_inc(result_stored, 16)
            sp.wait_ge(result_stored, 16 * (CH + 1))

        @block.gpsimd
        def _(pool):
            pool.memset(x_sb[:, BLOCKS - 1, :], 0.0).then_inc(pads_set, 1)
            for rows in (src_rows, dst_rows, type_rows):
                pool.memset(rows[:, FULL_SLABS, :], 0).then_inc(pads_set, 1)
            pool.memset(ident[:, :], 0.0).then_inc(ident_made, 1)
            pool.wait_ge(ident_made, 1)
            pool.affine_select(out=ident[:, :], in_=ident[:, :], compare_op=ALU.not_equal, fill=1.0,
                               base=0, pattern=[[-1, P]], channel_multiplier=1).then_inc(ident_made, 1)
            pool.wait_ge(edges_landed, 16 * EDGE_DMAS)
            pool.tensor_scalar(row_rows[:, :, :], type_rows[:, :, :], float(REL_EDGE), float(NPAD),
                               ALU.is_ge, ALU.mult).then_inc(rows_made, 1)
            pool.tensor_scalar(shift_rows[:, :, :], type_rows[:, :, :], float(2 * REL_EDGE), float(NPAD),
                               ALU.is_ge, ALU.mult).then_inc(rows_made, 1)
            pool.wait_ge(rows_made, 2)
            pool.tensor_tensor(row_rows[:, :, :], row_rows[:, :, :], shift_rows[:, :, :], ALU.add).then_inc(rows_made, 1)
            pool.wait_ge(rows_made, 3)
            pool.tensor_tensor(row_rows[:, :, :], row_rows[:, :, :], src_rows[:, :, :], ALU.add).then_inc(rows_made, 1)
            pool.wait_ge(rows_made, 4)
            pool.tensor_copy(rowf_rows[:, :, :], row_rows[:, :, :]).then_inc(rows_made, 1)
            pool.iota(iota[:, :], [[1, NPAD]], base=0, channel_multiplier=0,
                      allow_small_or_imprecise_dtypes=True).then_inc(iota_made, 1)
            pool.memset(msg[:, :, :, D:DA], 1.0).then_inc(ones_set, 1)
            pool.memset(sums[:, :, :], 0.0).then_inc(sums_zeroed, 1)

            def gather(slot, j, rows, landed):
                pool.indirect_dma_start(
                    msg[0:rows, slot, j, 0:D], None, table,
                    bass.IndirectOffsetOnAxis(ap=idx_ring[0:rows, slot, j:j + 1], axis=0)).then_inc(landed, 16)

            for i in range(YBUF):
                pool.wait_ge(y_stored[i], 16 * len(range(i, BLOCKS, YBUF)))
            with pool.Fori(0, GROUPS // RING) as r:
                for s in range(RING):
                    pool.wait_ge(idx_copied, r * RING + s + 1)
                    pool.wait_ge(slots_free, r * RING + s + 1)
                    pool.sem_inc(groups_begun, 1)
                    for j in range(GROUP):
                        gather(s, j, P, gathered[s])
            pool.wait_ge(slots_free, GROUPS + 1)
            pool.wait_ge(idx_copied, GROUPS + 1)
            for j in range(TAIL):
                gather(0, j, P if j < TAIL - 1 else LAST_EDGES, tail_gathered)

        @block.scalar
        def _(act):
            act.dma_start(w_sb[:, :, :], W.rearrange("g k f -> k g f")).then_inc(consts_landed, 16)
            for i in range(3):
                act.dma_start(b3[i:i + 1, :], b.rearrange("(a g) f -> a (g f)", a=1)).then_inc(consts_landed, 16)
            act.wait_ge(pads_set, 1)
            for c in range(CH):
                w0, w1 = c * XCH, (c + 1) * XCH
                if c < CH - 1:
                    act.dma_start(x_sb[:, w0:w1, :], x_blocks[:, w0:w1, :]).then_inc(x_landed[c], 16)
                else:
                    act.dma_start(x_sb[:, w0:w1 - 1, :], x_blocks[:, w0:w1 - 1, :]).then_inc(x_landed[c], 16)
                    act.dma_start(x_sb[0:LAST_ROWS, w1 - 1, :], x[N - LAST_ROWS:N, :]).then_inc(x_landed[c], 16)
            for w in range(BLOCKS + 1):
                if w < BLOCKS and w % XCH == 0:
                    c = w // XCH
                    act.wait_ge(var_made, c + 1)
                    act.activation(std[:, w:w + XCH], var_eps[:, w:w + XCH], ACT.Sqrt).then_inc(std_made, 1)
                if w < BLOCKS:
                    act.wait_ge(turned, w + 1)
                    if w >= 2:
                        act.wait_ge(projected, w - 1)
                    act.activation(hT[:, w % 2, :], ps_t[w % 2][:, :], ACT.Relu).then_inc(relu_made, 1)
                if w >= 1:
                    v = w - 1
                    act.wait_ge(projected, v + 1)
                    if v >= YBUF:
                        act.wait_ge(y_stored[v % YBUF], 16 * (v // YBUF))
                    act.activation(y_sb[:, v % YBUF, :], ps_y[v % 2][:, :], ACT.Copy).then_inc(y_copied, 1)
            act.wait_ge(edges_copied, 2 * SLABS_E)
            with act.Fori(0, GROUPS // RING) as r:
                for s in range(RING):
                    act.wait_ge(gathered[s], r * (16 * GROUP))
                    act.activation(idx_ring[:, s, :], row_idx[:, bass.ds((r * RING + s) * GROUP, GROUP)],
                                   ACT.Copy).then_inc(idx_copied, 1)
            act.wait_ge(gathered[0], GROUPS // RING * (16 * GROUP))
            act.activation(idx_ring[:, 0, 0:TAIL], row_idx[:, GROUPS * GROUP:TILES], ACT.Copy).then_inc(idx_copied, 1)
            act.wait_ge(rdeg_made, 2)
            for w in range(BLOCKS):
                if w >= XCH:
                    act.wait_ge(result_made, w // XCH)
                act.activation(mean[:, w % XCH, :], sums[:, w, 0:D], ACT.Relu,
                               scale=rdeg[:, w:w + 1]).then_inc(mean_made, 1)

        @block.tensor
        def _(pe):
            pe.wait_ge(ident_made, 2)

            def turn_edges(k, rows):
                if k >= 2:
                    pe.wait_ge(edges_copied, k - 1)
                k0 = (k % SLABS_E) * TPP
                n = min(TPP, SLABS - k0)
                for i in range(n):
                    last = pe.transpose(ps_e[k % 2][:, i * P:(i + 1) * P], rows[:, k0 + i, :], ident[:, :])
                last.then_inc(edges_turned, 1)

            pe.wait_ge(ends_made, 1)
            for k in range(SLABS_E):
                turn_edges(k, dstf_rows)
            pe.wait_ge(rows_made, 5)
            for k in range(SLABS_E, 2 * SLABS_E):
                turn_edges(k, rowf_rows)
            pe.wait_ge(ends_made, 3)
            n = 2 * SLABS_E
            for m, ends in enumerate((tile_min, tile_max)):
                for k in range(SLABS_E):
                    pe.wait_ge(edges_copied, n - 1)
                    k0 = k * TPP
                    for i in range(min(TPP, SLABS - k0)):
                        last = pe.matmul(ps_e[n % 2][0:1, i * P:(i + 1) * P], ends[:, k0 + i:k0 + i + 1],
                                         ident[:, :], start=True, stop=True)
                    last.then_inc(edges_turned, 1)
                    n += 1

            pe.wait_ge(consts_landed, 64)
            pe.wait_ge(b_steps, 9)
            for w in range(BLOCKS + 1):
                if w < BLOCKS:
                    pe.wait_ge(centred, w + 1)
                    if w >= 2:
                        pe.wait_ge(relu_made, w - 1)
                    pe.transpose(ps_t[w % 2][:, :], normed[:, w % 4, :], ident[:, :]).then_inc(turned, 1)
                if w >= 1:
                    v = w - 1
                    if v >= 2:
                        pe.wait_ge(y_copied, v - 1)
                    pe.matmul(ps_y[v % 2][:, :], ones3[:, :], b_split[:, :], start=True, stop=False)
                    pe.wait_ge(relu_made, v + 1)
                    pe.matmul(ps_y[v % 2][:, :], hT[:, v % 2, :], w_sb[:, :, :].rearrange("k g f -> k (g f)"),
                              start=False, stop=True).then_inc(projected, 1)

            def sum_windows(g, slot, landed, level, tiles, last_rows):
                count = pe.value_load(plan[0:1, bass.ds(g, 1), 1:2], min_val=1, max_val=BLOCKS)
                before = pe.value_load(plan[0:1, bass.ds(g, 1), 2:3], min_val=0, max_val=NG * BLOCKS)
                with pe.Fori(0, count) as i:
                    pe.wait_ge(onehot_made, before + i + 1)
                    pe.wait_ge(landed, level)
                    for j in range(tiles):
                        rows = P if j < tiles - 1 else last_rows
                        last = pe.matmul(ps_sum[:, :], onehot[0:rows, j, :], msg[0:rows, slot, j, :],
                                         start=(j == 0), stop=(j == tiles - 1))
                    last.then_inc(window_summed, 1)

            pe.wait_ge(plan_made, 1)
            pe.wait_ge(ones_set, 1)
            with pe.Fori(0, GROUPS // RING) as r:
                for s in range(RING):
                    sum_windows(r * RING + s, s, gathered[s], (r + 1) * (16 * GROUP), GROUP, P)
            sum_windows(GROUPS, 0, tail_gathered, 16 * TAIL, TAIL, LAST_EDGES)

        @block.vector
        def _(dve):
            dve.memset(ones3[:, :], 1.0).then_inc(b_steps, 1)
            dve.wait_ge(consts_landed, 64)
            dve.wait_ge(ident_made, 2)
            dve.tensor_copy(b_part[:, 0, :], b3[:, :]).then_inc(b_steps, 1)
            dve.wait_ge(b_steps, 2)
            dve.tensor_tensor(b_rest[:, :], b3[:, :], b_part[:, 0, :], ALU.subtract).then_inc(b_steps, 1)
            dve.wait_ge(b_steps, 3)
            dve.tensor_copy(b_part[:, 1, :], b_rest[:, :]).then_inc(b_steps, 1)
            dve.wait_ge(b_steps, 4)
            dve.tensor_tensor(b_part[:, 2, :], b_rest[:, :], b_part[:, 1, :], ALU.subtract).then_inc(b_steps, 1)
            dve.wait_ge(b_steps, 5)
            dve.tensor_scalar(b_sum[:, :], b_part[:, 0, :], ident[0:3, 0:1], None, ALU.mult).then_inc(b_steps, 1)
            for i in (1, 2):
                dve.wait_ge(b_steps, 5 + i)
                dve.scalar_tensor_tensor(out=b_sum[:, :], in0=b_part[:, i, :], scalar=ident[0:3, i:i + 1],
                                         in1=b_sum[:, :], op0=ALU.mult, op1=ALU.add).then_inc(b_steps, 1)
            dve.wait_ge(b_steps, 8)
            dve.tensor_copy(b_split[:, :], b_sum[:, :]).then_inc(b_steps, 1)

            dve.wait_ge(edges_landed, 16 * EDGE_DMAS)
            dve.tensor_copy(dstf_rows[:, :, :], dst_rows[:, :, :]).then_inc(ends_made, 1)
            dve.wait_ge(ends_made, 1)
            dve.tensor_reduce(tile_min[:, :], dstf_rows[:, :, :], AX_X, ALU.min).then_inc(ends_made, 1)
            dve.tensor_reduce(tile_max[:, :], dstf_rows[:, :, :], AX_X, ALU.max).then_inc(ends_made, 1)
            for k in range(2 * SLABS_E):
                to = dst_col if k < SLABS_E else row_idx
                k0 = (k % SLABS_E) * TPP * P
                n = min(TPP * P, SLABS * P - k0)
                dve.wait_ge(edges_turned, k + 1)
                dve.tensor_copy(to[:, k0:k0 + n], ps_e[k % 2][:, 0:n]).then_inc(edges_copied, 1)
            k = 2 * SLABS_E
            for m, op in enumerate((ALU.min, ALU.max)):
                for kk in range(SLABS_E):
                    t0 = kk * TPP * P
                    tiles = min(TPP * P, GROUPS * GROUP - t0)
                    dve.wait_ge(edges_turned, k + 1)
                    last = dve.tensor_reduce(edge_ends[:, m, t0 // GROUP:(t0 + tiles) // GROUP],
                                             ps_e[k % 2][0:1, 0:tiles].rearrange("a (g j) -> a g j", j=GROUP), AX_X, op)
                    if kk == SLABS_E - 1:
                        last = dve.tensor_reduce(edge_ends[:, m, GROUPS:NG],
                                                 ps_e[k % 2][0:1, tiles:tiles + TAIL], AX_X, op)
                    last.then_inc(edges_copied, 1)
                    k += 1
            def step(ins):
                plan_count[0] += 1
                ins.then_inc(plan_steps, 1)
                dve.wait_ge(plan_steps, plan_count[0])
            plan_count = [0]
            dve.wait_ge(edges_copied, k)
            step(dve.tensor_scalar(ends_int[:, :, :], edge_ends[:, :, :], 0.0, float(N - 1), ALU.max, ALU.min))
            step(dve.tensor_scalar(win_ends[:, :, :], ends_int[:, :, :], P.bit_length() - 1, None, ALU.logical_shift_right))
            step(dve.tensor_tensor(win_count[:, :], win_ends[:, 1, :], win_ends[:, 0, :], ALU.subtract))
            step(dve.tensor_scalar(win_count[:, :], win_count[:, :], 1.0, None, ALU.add))
            step(dve.memset(zeros1[:, :], 0.0))
            step(dve.tensor_tensor_scan(win_upto[:, :], win_count[:, :], zeros1[:, :], 0.0, ALU.add, ALU.add))
            step(dve.tensor_tensor(win_upto[:, :], win_upto[:, :], win_count[:, :], ALU.subtract))
            step(dve.tensor_copy(plan[:, :, 0], win_ends[:, 0, :]))
            step(dve.tensor_copy(plan[:, :, 1], win_count[:, :]))
            dve.tensor_copy(plan[:, :, 2], win_upto[:, :]).then_inc(plan_made, 1)

            for c in range(CH):
                w0, w1 = c * XCH, (c + 1) * XCH
                dve.wait_ge(x_landed[c], 16 if c < CH - 1 else 32)
                if c >= 1:
                    dve.wait_ge(stats_made, c * 2 * XCH)
                for w in range(w0, w1):
                    dve.bn_stats(stats[:, w - w0, :], x_sb[:, w, :]).then_inc(stats_made, 1)
                for w in range(w0, w1):
                    dve.wait_ge(stats_made, c * 2 * XCH + XCH + 0)
                    dve.bn_aggr(mv[:, w, :], stats[:, w - w0, :]).then_inc(stats_made, 1)
                dve.wait_ge(stats_made, (c + 1) * 2 * XCH)
                dve.tensor_scalar(var_eps[:, w0:w1], mv[:, w0:w1, 1], EPS, None, ALU.add).then_inc(var_made, 1)
                dve.wait_ge(std_made, c + 1)
                dve.reciprocal(rstd[:, w0:w1], std[:, w0:w1]).then_inc(rstd_made, 1)
                dve.wait_ge(rstd_made, c + 1)
                for w in range(w0, w1):
                    if w >= 4:
                        dve.wait_ge(turned, w - 3)
                    dve.tensor_scalar(normed[:, w % 4, :], x_sb[:, w, :], mv[:, w, 0:1], rstd[:, w:w + 1],
                                      ALU.subtract, ALU.mult).then_inc(centred, 1)

            def add_windows(g, tiles):
                first = dve.value_load(plan[0:1, bass.ds(g, 1), 0:1], min_val=0, max_val=BLOCKS - 1)
                count = dve.value_load(plan[0:1, bass.ds(g, 1), 1:2], min_val=1, max_val=BLOCKS)
                before = dve.value_load(plan[0:1, bass.ds(g, 1), 2:3], min_val=0, max_val=NG * BLOCKS)
                with dve.Fori(0, count) as i:
                    w = nc.s_assert_within(first + i, 0, BLOCKS - 1, skip_runtime_bounds_check_because=
                                           "the plan's windows end at the last one: the dst behind it are clamped")
                    dve.tensor_tensor(
                        onehot[:, 0:tiles, :],
                        dst_col[:, bass.ds(g * GROUP, tiles)].unsqueeze(2).to_broadcast([P, tiles, P]),
                        iota[:, bass.ds(w * P, P)].unsqueeze(1).to_broadcast([P, tiles, P]),
                        ALU.is_equal).then_inc(onehot_made, 1)
                    dve.wait_ge(window_summed, before + i + 1)
                    where = sums[:, bass.ds(w, 1), :].rearrange("p a f -> p (a f)")
                    dve.tensor_tensor(where, where, ps_sum[:, :], ALU.add).then_inc(window_added, 1)
                    dve.wait_ge(window_added, before + i + 1)

            dve.wait_ge(plan_made, 1)
            dve.wait_ge(iota_made, 1)
            dve.wait_ge(sums_zeroed, 1)
            dve.sem_inc(slots_free, RING)
            with dve.Fori(0, GROUPS // RING) as r:
                for s in range(RING):
                    add_windows(r * RING + s, GROUP)
                    dve.sem_inc(slots_free, 1)
            add_windows(GROUPS, TAIL)

            dve.tensor_scalar(deg[:, :], sums[:, :, D], 1.0, None, ALU.max).then_inc(rdeg_made, 1)
            dve.wait_ge(rdeg_made, 1)
            dve.reciprocal(rdeg[:, :], deg[:, :]).then_inc(rdeg_made, 1)
            for c in range(CH):
                dve.wait_ge(mean_made, (c + 1) * XCH)
                dve.tensor_tensor(x_sb[:, c * XCH:(c + 1) * XCH, :], mean[:, :, :],
                                  x_sb[:, c * XCH:(c + 1) * XCH, :], ALU.add).then_inc(result_made, 1)


_INS = ['x', 'src', 'dst', 'edge_type_30', 'L0_gnn_W', 'L0_gnn_b']
_OUTS = [((6250, 128), 'float32')]


def kernel(**inputs):
    import numpy as _np
    import concourse.bacc as _bacc
    from concourse import mybir as _mybir
    from concourse.bass_utils import run_bass_kernel_spmd as _run

    nc = _bacc.Bacc("TRN2", target_bir_lowering=False, num_devices=1)
    arrays, args = {}, []
    for name in _INS:
        a = _np.ascontiguousarray(inputs[name])
        arrays[f"in_{name}_dram"] = a
        args.append(nc.dram_tensor(f"in_{name}_dram", a.shape, _mybir.dt.from_np(a.dtype), kind="ExternalInput").ap())
    for i, (shape, dtype) in enumerate(_OUTS):
        dt = _mybir.dt.from_np(_np.dtype(dtype))
        args.append(nc.dram_tensor(f"out_{i}_dram", shape, dt, kind="ExternalOutput").ap())
    bass_gnn_mean_aggregate_kernel(nc, *args)
    r = _run(nc, [arrays], core_ids=[0])
    got = tuple(r.results[0][f"out_{i}_dram"] for i in range(len(_OUTS)))
    return got[0]
```

```python
from contextlib import ExitStack

import concourse.bass as bass
from concourse import mybir

F32 = mybir.dt.float32
BF16 = mybir.dt.bfloat16
I32 = mybir.dt.int32
ALU = mybir.AluOpType
ACT = mybir.ActivationFunctionType
AX_X = mybir.AxisListType.X

P = 128
GROUP = 8
RING = 3
REL_EDGE = 10
EPS = 1e-5
YBUF = 4


def bass_gnn_mean_aggregate_kernel(
    nc: bass.Bass,
    x: bass.AP,
    src: bass.AP,
    dst: bass.AP,
    edge_type: bass.AP,
    W: bass.AP,
    b: bass.AP,
    out: bass.AP,
):
    N, D = x.shape
    E = src.shape[0]
    R = W.shape[0]
    RD = R * D
    BLOCKS = -(-N // P)
    NPAD = BLOCKS * P
    LAST_ROWS = N - (BLOCKS - 1) * P
    TILES = -(-E // P)
    LAST_EDGES = E - (TILES - 1) * P
    GROUPS = TILES // GROUP
    TAIL = TILES - GROUPS * GROUP
    assert GROUPS % RING == 0 and 0 < TAIL < GROUP and D == P
    SLABS = -(-TILES // P)
    FULL_SLABS = TILES // P
    REST_TILES = TILES - FULL_SLABS * P - 1
    DA = D + 1
    NBUF = 8
    ROWS_AT, DST_AT = 2, 5
    DVE_SHARE = 2
    TPP = 4
    XCH = 7
    SLABS_E = -(-SLABS // TPP)
    assert BLOCKS % XCH == 0
    CH = BLOCKS // XCH

    table = nc.dram_tensor("node_table", (R * NPAD, D), F32, kind="Internal").ap()

    with ExitStack() as ctx:
        def sb(name, shape, dt):
            return ctx.enter_context(nc.sbuf_tensor(name, shape, dt))

        def ps(name, shape, dt=F32):
            return ctx.enter_context(nc.psum_tensor(name, shape, dt))

        def sem(name):
            return ctx.enter_context(nc.semaphore(name))

        x_sb = sb("x_sb", [P, BLOCKS, D], F32)
        stats = sb("stats", [P, BLOCKS, 6], F32)
        mv = sb("mv", [P, BLOCKS, 2], F32)
        var_eps = sb("var_eps", [P, BLOCKS], F32)
        std = sb("std", [P, BLOCKS], F32)
        rstd = sb("rstd", [P, BLOCKS], F32)
        normed = sb("normed", [P, NBUF, D], F32)
        hT = sb("hT", [P, 2, P], F32)
        y_sb = sb("y_sb", [P, YBUF, RD], F32)
        w_sb = sb("w_sb", [P, R, D], F32)
        b3 = sb("b3", [3, RD], F32)
        b_rest = sb("b_rest", [3, RD], F32)
        b_part = sb("b_part", [3, 3, RD], BF16)
        b_sum = sb("b_sum", [3, RD], F32)
        b_split = sb("b_split", [3, RD], BF16)
        ones3 = sb("ones3", [3, P], BF16)
        ident = sb("ident", [P, P], F32)
        src_rows = sb("src_rows", [P, SLABS, P], I32)
        dst_rows = sb("dst_rows", [P, SLABS, P], I32)
        type_rows = sb("type_rows", [P, SLABS, P], I32)
        rel_rows = sb("rel_rows", [P, SLABS, P], F32)
        row_rows = sb("row_rows", [P, SLABS, P], F32)
        dstf_rows = sb("dstf_rows", [P, SLABS, P], F32)
        row_idx = sb("row_idx", [P, SLABS * P], I32)
        idx_ring = sb("idx_ring", [P, RING, GROUP], I32)
        dst_col = sb("dst_col", [P, SLABS * P], F32)
        tile_min = sb("tile_min", [P, SLABS], F32)
        tile_max = sb("tile_max", [P, SLABS], F32)
        NG = GROUPS + 1
        edge_ends = sb("edge_ends", [1, 2, NG], F32)
        ends_int = sb("ends_int", [1, 2, NG], I32)
        win_ends = sb("win_ends", [1, 2, NG], I32)
        win_count = sb("win_count", [1, NG], F32)
        extras = sb("extras", [1, NG], F32)
        extras_upto = sb("extras_upto", [1, NG], F32)
        zeros1 = sb("zeros1", [1, NG], F32)
        plan = sb("plan", [1, NG, 3], I32)
        iota = sb("iota", [P, NPAD], F32)
        onehot = sb("onehot", [P, RING, GROUP, P], F32)
        onehot_x = sb("onehot_x", [P, GROUP, P], F32)
        msg = sb("msg", [P, RING, GROUP, DA], F32)
        sums = sb("sums", [P, BLOCKS, DA], F32)
        deg = sb("deg", [P, BLOCKS], F32)
        rdeg = sb("rdeg", [P, BLOCKS], F32)

        ps_t = [ps(f"ps_t{i}", [P, P]) for i in range(2)]
        ps_y = [ps(f"ps_y{i}", [P, RD]) for i in range(2)]
        ps_e = [ps(f"ps_e{i}", [P, TPP * P]) for i in range(2)]
        ps_first = [bank[:, 0:DA] for bank in (ps_y[0], ps_y[1], ps_e[0])]
        ps_x = ps("ps_x", [P, DA])

        x_landed = [sem(f"x_landed{c}") for c in range(CH)]
        pads_set = sem("pads_set")
        rows_landed = sem("rows_landed")
        dst_landed = sem("dst_landed")
        consts_landed = sem("consts_landed")
        ident_made = sem("ident_made")
        iota_made = sem("iota_made")
        rows_made = sem("rows_made")
        rows_turned = sem("rows_turned")
        rows_copied = sem("rows_copied")
        b_steps = sem("b_steps")
        ends_made = sem("ends_made")
        stats_made = sem("stats_made")
        mv_made = sem("mv_made")
        var_made = sem("var_made")
        std_made = sem("std_made")
        rstd_made = sem("rstd_made")
        centred = sem("centred")
        turned = sem("turned")
        relu_made = sem("relu_made")
        projected = sem("projected")
        y_copied = sem("y_copied")
        y_stored = [sem(f"y_stored{i}") for i in range(YBUF)]
        edges_turned = sem("edges_turned")
        edges_copied = sem("edges_copied")
        ends_turned = sem("ends_turned")
        ends_reduced = sem("ends_reduced")
        plan_steps = sem("plan_steps")
        plan_made = sem("plan_made")
        ones_set = sem("ones_set")
        sums_zeroed = sem("sums_zeroed")
        gathered = [sem(f"gathered{i}") for i in range(RING)]
        tail_gathered = sem("tail_gathered")
        groups_begun = sem("groups_begun")
        idx_copied = sem("idx_copied")
        slots_free = sem("slots_free")
        first_added = sem("first_added")
        extra_added = sem("extra_added")
        onehot_made = sem("onehot_made")
        first_summed = sem("first_summed")
        extra_made = sem("extra_made")
        extra_summed = sem("extra_summed")
        rdeg_made = sem("rdeg_made")
        mean_made = sem("mean_made")
        mean_scaled = sem("mean_scaled")
        result_made = sem("result_made")
        result_stored = sem("result_stored")

        block = ctx.enter_context(nc.Block())

        x_blocks = x[0:(BLOCKS - 1) * P, :].rearrange("(w p) f -> p w f", p=P)
        out_blocks = out[0:(BLOCKS - 1) * P, :].rearrange("(w p) f -> p w f", p=P)
        table_rows = table.rearrange("(g w p) f -> w p g f", g=R, p=P)
        PADS = 4

        def edge_loads(eng, sb_rows, dram, twice, landed):
            eng.dma_start(sb_rows[:, 0:FULL_SLABS, :],
                          dram[0:FULL_SLABS * P * P].rearrange("(s p e) -> p s e", p=P, e=P)).then_inc(landed, 16)
            rest = FULL_SLABS * P * P
            eng.dma_start(sb_rows[0:REST_TILES, FULL_SLABS, :],
                          dram[rest:rest + REST_TILES * P].rearrange("(p e) -> p e", e=P)).then_inc(landed, 16)
            last = dram[E - LAST_EDGES:E].rearrange("(a e) -> a e", a=1)
            eng.dma_start(sb_rows[REST_TILES:REST_TILES + 1, FULL_SLABS, 0:LAST_EDGES], last).then_inc(landed, 16)
            if twice:
                eng.dma_start(sb_rows[REST_TILES:REST_TILES + 1, FULL_SLABS, LAST_EDGES:2 * LAST_EDGES],
                              last).then_inc(landed, 16)
        assert 2 * LAST_EDGES == P

        @block.sync
        def _(sp):
            sp.wait_ge(pads_set, PADS)
            for c in range(CH):
                w0, w1 = c * XCH, (c + 1) * XCH
                if c < CH - 1:
                    sp.dma_start(x_sb[:, w0:w1, :], x_blocks[:, w0:w1, :]).then_inc(x_landed[c], 16)
                else:
                    sp.dma_start(x_sb[:, w0:w1 - 1, :], x_blocks[:, w0:w1 - 1, :]).then_inc(x_landed[c], 16)
                    sp.dma_start(x_sb[0:LAST_ROWS, w1 - 1, :], x[N - LAST_ROWS:N, :]).then_inc(x_landed[c], 16)
                if c == 1:
                    edge_loads(sp, type_rows, edge_type, False, rows_landed)
                    edge_loads(sp, src_rows, src, False, rows_landed)
                if c == 3:
                    edge_loads(sp, dst_rows, dst, True, dst_landed)
            for w in range(BLOCKS):
                sp.wait_ge(y_copied, w + 1)
                sp.dma_start(table_rows[w], y_sb[:, w % YBUF, :].rearrange("p (g f) -> p g f", g=R)).then_inc(
                    y_stored[w % YBUF], 16)
            for c in range(CH):
                sp.wait_ge(result_made, c + 1)
                w0, w1 = c * XCH, (c + 1) * XCH
                if c < CH - 1:
                    sp.dma_start(out_blocks[:, w0:w1, :], x_sb[:, w0:w1, :]).then_inc(result_stored, 16)
                else:
                    sp.dma_start(out_blocks[:, w0:w1 - 1, :], x_sb[:, w0:w1 - 1, :]).then_inc(result_stored, 16)
                    sp.dma_start(out[N - LAST_ROWS:N, :], x_sb[0:LAST_ROWS, w1 - 1, :]).then_inc(result_stored, 16)
            sp.wait_ge(result_stored, 16 * (CH + 1))

        @block.gpsimd
        def _(pool):
            pool.memset(x_sb[:, BLOCKS - 1, :], 0.0).then_inc(pads_set, 1)
            for rows in (src_rows, dst_rows, type_rows):
                pool.memset(rows[:, FULL_SLABS, :], 0).then_inc(pads_set, 1)
            pool.memset(ident[:, :], 0.0).then_inc(ident_made, 1)
            pool.wait_ge(ident_made, 1)
            pool.affine_select(out=ident[:, :], in_=ident[:, :], compare_op=ALU.not_equal, fill=1.0,
                               base=0, pattern=[[-1, P]], channel_multiplier=1).then_inc(ident_made, 1)
            pool.iota(iota[:, :], [[1, NPAD]], base=0, channel_multiplier=0,
                      allow_small_or_imprecise_dtypes=True).then_inc(iota_made, 1)
            pool.memset(msg[:, :, :, D:DA], 1.0).then_inc(ones_set, 1)
            pool.memset(sums[:, :, :], 0.0).then_inc(sums_zeroed, 1)

            def gather(slot, j, rows, landed):
                pool.indirect_dma_start(
                    msg[0:rows, slot, j, 0:D], None, table,
                    bass.IndirectOffsetOnAxis(ap=idx_ring[0:rows, slot, j:j + 1], axis=0)).then_inc(landed, 16)

            for i in range(YBUF):
                pool.wait_ge(y_stored[i], 16 * len(range(i, BLOCKS, YBUF)))
            pool.sem_inc(slots_free, RING)
            with pool.Fori(0, GROUPS // RING) as r:
                for s in range(RING):
                    pool.wait_ge(idx_copied, r * RING + s + 1)
                    pool.wait_ge(slots_free, r * RING + s + 1)
                    pool.sem_inc(groups_begun, 1)
                    for j in range(GROUP):
                        gather(s, j, P, gathered[s])
            pool.wait_ge(slots_free, GROUPS + 1)
            pool.wait_ge(idx_copied, GROUPS + 1)
            for j in range(TAIL):
                gather(0, j, P if j < TAIL - 1 else LAST_EDGES, tail_gathered)

        @block.scalar
        def _(act):
            act.dma_start(w_sb[:, :, :], W.rearrange("g k f -> k g f")).then_inc(consts_landed, 16)
            for i in range(3):
                act.dma_start(b3[i:i + 1, :], b.rearrange("(a g) f -> a (g f)", a=1)).then_inc(consts_landed, 16)
            for w in range(BLOCKS + 1):
                if w < BLOCKS and w % XCH == 0:
                    for c in ([0, 1] if w == 0 else [w // XCH + 1] if w // XCH + 1 < CH else []):
                        act.wait_ge(var_made, c + 1)
                        act.activation(std[:, c * XCH:(c + 1) * XCH], var_eps[:, c * XCH:(c + 1) * XCH],
                                       ACT.Sqrt).then_inc(std_made, 1)
                if w < BLOCKS:
                    act.wait_ge(turned, w + 1)
                    if w >= 2:
                        act.wait_ge(projected, w - 1)
                    act.activation(hT[:, w % 2, :], ps_t[w % 2][:, :], ACT.Relu).then_inc(relu_made, 1)
                if w >= 1:
                    v = w - 1
                    act.wait_ge(projected, v + 1)
                    if v >= YBUF:
                        act.wait_ge(y_stored[v % YBUF], 16 * (v // YBUF))
                    act.activation(y_sb[:, v % YBUF, :], ps_y[v % 2][:, :], ACT.Copy).then_inc(y_copied, 1)
            act.wait_ge(rows_copied, SLABS_E)
            with act.Fori(0, GROUPS // RING) as r:
                for s in range(RING):
                    act.wait_ge(slots_free, r * RING + s + 1)
                    act.activation(idx_ring[:, s, :], row_idx[:, bass.ds((r * RING + s) * GROUP, GROUP)],
                                   ACT.Copy).then_inc(idx_copied, 1)
            act.wait_ge(slots_free, GROUPS + 1)
            act.activation(idx_ring[:, 0, 0:TAIL], row_idx[:, GROUPS * GROUP:TILES], ACT.Copy).then_inc(idx_copied, 1)
            act.wait_ge(rdeg_made, 2)
            for c in range(CH):
                for w in range(c * XCH + DVE_SHARE, (c + 1) * XCH):
                    last = act.activation(sums[:, w, 0:D], sums[:, w, 0:D], ACT.Relu, scale=rdeg[:, w:w + 1])
                last.then_inc(mean_made, 1)

        @block.tensor
        def _(pe):
            pe.wait_ge(ident_made, 2)

            def turn(rows, turned_sem, copied_sem):
                for k in range(SLABS_E):
                    if k >= 2:
                        pe.wait_ge(copied_sem, k - 1)
                    for i in range(min(TPP, SLABS - k * TPP)):
                        last = pe.transpose(ps_e[k % 2][:, i * P:(i + 1) * P], rows[:, k * TPP + i, :], ident[:, :])
                    last.then_inc(turned_sem, 1)

            def turn_ends():
                for m, ends in enumerate((tile_min, tile_max)):
                    for k in range(SLABS_E):
                        n = m * SLABS_E + k
                        if n < 2:
                            pe.wait_ge(edges_copied, SLABS_E)
                        else:
                            pe.wait_ge(ends_reduced, n - 1)
                        for i in range(min(TPP, SLABS - k * TPP)):
                            last = pe.matmul(ps_e[n % 2][0:1, i * P:(i + 1) * P],
                                             ends[:, k * TPP + i:k * TPP + i + 1], ident[:, :], start=True, stop=True)
                        last.then_inc(ends_turned, 1)

            pe.wait_ge(consts_landed, 64)
            for w in range(BLOCKS + 1):
                if w < BLOCKS:
                    pe.wait_ge(centred, w + 1)
                    if w >= 2:
                        pe.wait_ge(relu_made, w - 1)
                    pe.transpose(ps_t[w % 2][:, :], normed[:, w % NBUF, :], ident[:, :]).then_inc(turned, 1)
                if w >= 1:
                    v = w - 1
                    if v == 0:
                        pe.wait_ge(b_steps, 9)
                    if v >= 2:
                        pe.wait_ge(y_copied, v - 1)
                    pe.matmul(ps_y[v % 2][:, :], ones3[:, :], b_split[:, :], start=True, stop=False)
                    pe.wait_ge(relu_made, v + 1)
                    pe.matmul(ps_y[v % 2][:, :], hT[:, v % 2, :], w_sb[:, :, :].rearrange("k g f -> k (g f)"),
                              start=False, stop=True).then_inc(projected, 1)
                if w == ROWS_AT * XCH:
                    pe.wait_ge(rows_made, 3)
                    turn(row_rows, rows_turned, rows_copied)
                if w == DST_AT * XCH:
                    pe.wait_ge(rows_copied, SLABS_E)
                    pe.wait_ge(ends_made, 1)
                    turn(dstf_rows, edges_turned, edges_copied)
            pe.wait_ge(ends_made, 3)
            turn_ends()

            def sum_tiles(to, onehots, slot, tiles, last_rows):
                for j in range(tiles):
                    rows = P if j < tiles - 1 else last_rows
                    last = pe.matmul(to, onehots[0:rows, j, :], msg[0:rows, slot, j, :],
                                     start=(j == 0), stop=(j == tiles - 1))
                return last

            def sum_windows(g, slot, landed, level, tiles, last_rows):
                pe.wait_ge(onehot_made, g + 1)
                pe.wait_ge(landed, level)
                sum_tiles(ps_first[slot], onehot[:, slot, :, :], slot, tiles, last_rows).then_inc(first_summed, 1)
                count = pe.value_load(plan[0:1, bass.ds(g, 1), 1:2], min_val=1, max_val=BLOCKS)
                with pe.If(count > 1):
                    before = pe.value_load(plan[0:1, bass.ds(g, 1), 2:3], min_val=0, max_val=NG * BLOCKS)
                    with pe.Fori(1, count) as i:
                        pe.wait_ge(extra_made, before + i)
                        sum_tiles(ps_x[:, :], onehot_x, slot, tiles, last_rows).then_inc(extra_summed, 1)

            pe.wait_ge(plan_made, 1)
            pe.wait_ge(ones_set, 1)
            pe.wait_ge(y_copied, BLOCKS)
            with pe.Fori(0, GROUPS // RING) as r:
                for s in range(RING):
                    sum_windows(r * RING + s, s, gathered[s], (r + 1) * (16 * GROUP), GROUP, P)
            sum_windows(GROUPS, 0, tail_gathered, 16 * TAIL, TAIL, LAST_EDGES)

        @block.vector
        def _(dve):
            dve.memset(ones3[:, :], 1.0).then_inc(b_steps, 1)
            dve.wait_ge(consts_landed, 64)
            dve.wait_ge(ident_made, 2)
            dve.tensor_copy(b_part[:, 0, :], b3[:, :]).then_inc(b_steps, 1)
            dve.wait_ge(b_steps, 2)
            dve.tensor_tensor(b_rest[:, :], b3[:, :], b_part[:, 0, :], ALU.subtract).then_inc(b_steps, 1)
            dve.wait_ge(b_steps, 3)
            dve.tensor_copy(b_part[:, 1, :], b_rest[:, :]).then_inc(b_steps, 1)
            dve.wait_ge(b_steps, 4)
            dve.tensor_tensor(b_part[:, 2, :], b_rest[:, :], b_part[:, 1, :], ALU.subtract).then_inc(b_steps, 1)
            dve.wait_ge(b_steps, 5)
            dve.tensor_scalar(b_sum[:, :], b_part[:, 0, :], ident[0:3, 0:1], None, ALU.mult).then_inc(b_steps, 1)
            for i in (1, 2):
                dve.wait_ge(b_steps, 5 + i)
                dve.scalar_tensor_tensor(out=b_sum[:, :], in0=b_part[:, i, :], scalar=ident[0:3, i:i + 1],
                                         in1=b_sum[:, :], op0=ALU.mult, op1=ALU.add).then_inc(b_steps, 1)
            dve.wait_ge(b_steps, 8)
            dve.tensor_copy(b_split[:, :], b_sum[:, :]).then_inc(b_steps, 1)

            def norm_stats(c):
                w0, w1 = c * XCH, (c + 1) * XCH
                dve.wait_ge(x_landed[c], 16 if c < CH - 1 else 32)
                for w in range(w0, w1):
                    dve.bn_stats(stats[:, w, :], x_sb[:, w, :]).then_inc(stats_made, 1)
                dve.wait_ge(stats_made, w1)
                for w in range(w0, w1):
                    dve.bn_aggr(mv[:, w, :], stats[:, w, :]).then_inc(mv_made, 1)
                dve.wait_ge(mv_made, w1)
                dve.tensor_scalar(var_eps[:, w0:w1], mv[:, w0:w1, 1], EPS, None, ALU.add).then_inc(var_made, 1)

            def norm(c):
                w0, w1 = c * XCH, (c + 1) * XCH
                dve.wait_ge(std_made, c + 1)
                dve.reciprocal(rstd[:, w0:w1], std[:, w0:w1]).then_inc(rstd_made, 1)
                dve.wait_ge(rstd_made, c + 1)
                for w in range(w0, w1):
                    if w >= NBUF:
                        dve.wait_ge(turned, w - NBUF + 1)
                    dve.tensor_scalar(normed[:, w % NBUF, :], x_sb[:, w, :], mv[:, w, 0:1], rstd[:, w:w + 1],
                                      ALU.subtract, ALU.mult).then_inc(centred, 1)

            def edge_rows():
                dve.wait_ge(rows_landed, 16 * 6)
                dve.tensor_scalar(rel_rows[:, :, :], type_rows[:, :, :], float(2 * REL_EDGE), None,
                                  ALU.is_ge).then_inc(rows_made, 1)
                dve.wait_ge(rows_made, 1)
                dve.scalar_tensor_tensor(out=rel_rows[:, :, :], in0=type_rows[:, :, :], scalar=float(REL_EDGE),
                                         in1=rel_rows[:, :, :], op0=ALU.is_ge, op1=ALU.add).then_inc(rows_made, 1)
                dve.wait_ge(rows_made, 2)
                dve.scalar_tensor_tensor(out=row_rows[:, :, :], in0=rel_rows[:, :, :], scalar=float(NPAD),
                                         in1=src_rows[:, :, :], op0=ALU.mult, op1=ALU.add).then_inc(rows_made, 1)

            def copy_turned(to, turned_sem, copied_sem):
                for k in range(SLABS_E):
                    k0 = k * TPP * P
                    n = min(TPP * P, SLABS * P - k0)
                    dve.wait_ge(turned_sem, k + 1)
                    dve.tensor_copy(to[:, k0:k0 + n], ps_e[k % 2][:, 0:n]).then_inc(copied_sem, 1)

            def tile_ends():
                dve.wait_ge(dst_landed, 16 * 4)
                dve.tensor_copy(dstf_rows[:, :, :], dst_rows[:, :, :]).then_inc(ends_made, 1)
                dve.wait_ge(ends_made, 1)
                dve.tensor_reduce(tile_min[:, :], dstf_rows[:, :, :], AX_X, ALU.min).then_inc(ends_made, 1)
                dve.tensor_reduce(tile_max[:, :], dstf_rows[:, :, :], AX_X, ALU.max).then_inc(ends_made, 1)

            norm_stats(0)
            for c in range(CH):
                if c + 1 < CH:
                    norm_stats(c + 1)
                norm(c)
                if c == ROWS_AT - 1:
                    edge_rows()
                if c == ROWS_AT:
                    copy_turned(row_idx, rows_turned, rows_copied)
                if c == DST_AT - 1:
                    tile_ends()
                if c == DST_AT:
                    copy_turned(dst_col, edges_turned, edges_copied)
            for m, op in enumerate((ALU.min, ALU.max)):
                for k in range(SLABS_E):
                    n = m * SLABS_E + k
                    t0 = k * TPP * P
                    tiles = min(TPP * P, GROUPS * GROUP - t0)
                    dve.wait_ge(ends_turned, n + 1)
                    last = dve.tensor_reduce(edge_ends[:, m, t0 // GROUP:(t0 + tiles) // GROUP],
                                             ps_e[n % 2][0:1, 0:tiles].rearrange("a (g j) -> a g j", j=GROUP), AX_X, op)
                    if k == SLABS_E - 1:
                        last = dve.tensor_reduce(edge_ends[:, m, GROUPS:NG],
                                                 ps_e[n % 2][0:1, tiles:tiles + TAIL], AX_X, op)
                    last.then_inc(ends_reduced, 1)
            def step(ins):
                plan_count[0] += 1
                ins.then_inc(plan_steps, 1)
                dve.wait_ge(plan_steps, plan_count[0])
            plan_count = [0]
            dve.wait_ge(ends_reduced, 2 * SLABS_E)
            step(dve.tensor_scalar(ends_int[:, :, :], edge_ends[:, :, :], 0.0, float(N - 1), ALU.max, ALU.min))
            step(dve.tensor_scalar(win_ends[:, :, :], ends_int[:, :, :], P.bit_length() - 1, None,
                                   ALU.logical_shift_right))
            step(dve.tensor_tensor(extras[:, :], win_ends[:, 1, :], win_ends[:, 0, :], ALU.subtract))
            step(dve.memset(zeros1[:, :], 0.0))
            step(dve.tensor_tensor_scan(extras_upto[:, :], extras[:, :], zeros1[:, :], 0.0, ALU.add, ALU.add))
            step(dve.tensor_copy(plan[:, :, 0], win_ends[:, 0, :]))
            step(dve.tensor_scalar(plan[:, :, 1], extras[:, :], 1.0, None, ALU.add))
            step(dve.tensor_tensor(plan[:, :, 2], extras_upto[:, :], extras[:, :], ALU.subtract))
            dve.sem_inc(plan_made, 1)

            def load_first(g):
                return dve.value_load(plan[0:1, bass.ds(g, 1), 0:1], min_val=0, max_val=BLOCKS - 1)

            def one_hots(to, g, w, made):
                dve.tensor_tensor(
                    to, dst_col[:, bass.ds(g * GROUP, GROUP)].unsqueeze(2).to_broadcast([P, GROUP, P]),
                    iota[:, bass.ds(w * P, P)].unsqueeze(1).to_broadcast([P, GROUP, P]),
                    ALU.is_equal).then_inc(made, 1)

            def add(bank, w, added):
                where = sums[:, bass.ds(w, 1), :].rearrange("p a f -> p (a f)")
                dve.tensor_tensor(where, where, bank, ALU.add).then_inc(added, 1)

            def add_windows(g, slot):
                first = load_first(g)
                count = dve.value_load(plan[0:1, bass.ds(g, 1), 1:2], min_val=1, max_val=BLOCKS)
                dve.wait_ge(first_summed, g + 1)
                add(ps_first[slot], first, first_added)
                with dve.If(count > 1):
                    before = dve.value_load(plan[0:1, bass.ds(g, 1), 2:3], min_val=0, max_val=NG * BLOCKS)
                    with dve.Fori(1, count) as i:
                        w = nc.s_assert_within(first + i, 0, BLOCKS - 1, skip_runtime_bounds_check_because=
                                               "the plan's windows end at the last one: the dst behind it are clamped")
                        one_hots(onehot_x[:, :, :], g, w, extra_made)
                        dve.wait_ge(extra_summed, before + i)
                        dve.wait_ge(first_added, g + 1)
                        add(ps_x[:, :], w, extra_added)
                        dve.wait_ge(extra_added, before + i)

            dve.wait_ge(iota_made, 1)
            dve.wait_ge(sums_zeroed, 1)
            one_hots(onehot[:, 0, :, :], 0, load_first(0), onehot_made)
            with dve.Fori(0, GROUPS // RING) as r:
                for s in range(RING):
                    nxt = (s + 1) % RING
                    one_hots(onehot[:, nxt, :, :], r * RING + s + 1, load_first(r * RING + s + 1), onehot_made)
                    add_windows(r * RING + s, s)
                    dve.wait_ge(first_added, r * RING + s + 1)
                    dve.sem_inc(slots_free, 1)
            add_windows(GROUPS, 0)
            dve.wait_ge(first_added, NG)

            dve.tensor_scalar(deg[:, :], sums[:, :, D], 1.0, None, ALU.max).then_inc(rdeg_made, 1)
            dve.wait_ge(rdeg_made, 1)
            dve.reciprocal(rdeg[:, :], deg[:, :]).then_inc(rdeg_made, 1)
            dve.wait_ge(rdeg_made, 2)
            for c in range(CH):
                w0, w1 = c * XCH, (c + 1) * XCH
                for w in range(w0, w0 + DVE_SHARE):
                    dve.tensor_scalar(sums[:, w, 0:D], sums[:, w, 0:D], rdeg[:, w:w + 1], 0.0,
                                      ALU.mult, ALU.max).then_inc(mean_scaled, 1)
                dve.wait_ge(mean_scaled, (c + 1) * DVE_SHARE)
                dve.wait_ge(mean_made, c + 1)
                dve.tensor_tensor(x_sb[:, w0:w1, :], sums[:, w0:w1, 0:D],
                                  x_sb[:, w0:w1, :], ALU.add).then_inc(result_made, 1)


_INS = ['x', 'src', 'dst', 'edge_type_30', 'L0_gnn_W', 'L0_gnn_b']
_OUTS = [((6250, 128), 'float32')]


def kernel(**inputs):
    import numpy as _np
    import concourse.bacc as _bacc
    from concourse import mybir as _mybir
    from concourse.bass_utils import run_bass_kernel_spmd as _run

    nc = _bacc.Bacc("TRN2", target_bir_lowering=False, num_devices=1)
    arrays, args = {}, []
    for name in _INS:
        a = _np.ascontiguousarray(inputs[name])
        arrays[f"in_{name}_dram"] = a
        args.append(nc.dram_tensor(f"in_{name}_dram", a.shape, _mybir.dt.from_np(a.dtype), kind="ExternalInput").ap())
    for i, (shape, dtype) in enumerate(_OUTS):
        dt = _mybir.dt.from_np(_np.dtype(dtype))
        args.append(nc.dram_tensor(f"out_{i}_dram", shape, dt, kind="ExternalOutput").ap())
    bass_gnn_mean_aggregate_kernel(nc, *args)
    r = _run(nc, [arrays], core_ids=[0])
    got = tuple(r.results[0][f"out_{i}_dram"] for i in range(len(_OUTS)))
    return got[0]
```

```python
from contextlib import ExitStack

import concourse.bass as bass
from concourse import mybir

F32 = mybir.dt.float32
BF16 = mybir.dt.bfloat16
I32 = mybir.dt.int32
ALU = mybir.AluOpType
ACT = mybir.ActivationFunctionType
AX_X = mybir.AxisListType.X

P = 128
GROUP = 8
RING = 13
EARLY = 7
REL_EDGE = 10
EPS = 1e-5
YBUF = 6


def bass_gnn_mean_aggregate_kernel(
    nc: bass.Bass,
    x: bass.AP,
    src: bass.AP,
    dst: bass.AP,
    edge_type: bass.AP,
    W: bass.AP,
    b: bass.AP,
    out: bass.AP,
):
    N, D = x.shape
    E = src.shape[0]
    R = W.shape[0]
    RD = R * D
    BLOCKS = -(-N // P)
    NPAD = BLOCKS * P
    LAST_ROWS = N - (BLOCKS - 1) * P
    TILES = -(-E // P)
    LAST_EDGES = E - (TILES - 1) * P
    GROUPS = TILES // GROUP
    TAIL = TILES - GROUPS * GROUP
    assert GROUPS % RING == 0 and 0 < TAIL < GROUP and D == P and EARLY < RING
    EARLY_TILES = EARLY * GROUP
    assert EARLY_TILES <= P
    ALL = BLOCKS + EARLY_TILES
    SLABS = -(-TILES // P)
    FULL_SLABS = TILES // P
    REST_TILES = TILES - FULL_SLABS * P - 1
    DA = D + 1
    NBUF = 8
    DVE_SHARE = 3
    BANK_SLABS = 4
    XCH = 7
    BANKS = -(-SLABS // BANK_SLABS)
    assert BLOCKS % XCH == 0
    ROWS_AT, ENDS_AT, DST_AT = 4 * XCH, 6 * XCH, BLOCKS + 1
    CH = BLOCKS // XCH
    CHUNKS = [(c * XCH, (c + 1) * XCH) for c in range(CH)]
    CHUNKS += [(BLOCKS + e * GROUP, BLOCKS + (e + 1) * GROUP) for e in range(EARLY)]
    FINISH_FROM = GROUPS - RING
    FINISH_BLOCKS = (CH - 1) * XCH
    ZEROED_FIRST, ZEROED_NEXT = BLOCKS // 3, 4 * BLOCKS // 7
    ROOT_LEAD = 3
    LAG = 5
    SUM_AT = 3
    ONEHOT_AT = 1
    assert SUM_AT - 1 + LAG < GROUP

    table = nc.dram_tensor("node_table", (R * NPAD, D), F32, kind="Internal").ap()

    with ExitStack() as ctx:
        SETS = 3

        def set_of(slot):
            return SETS - 1 if slot % RING == RING - 1 else slot % RING % 2

        def rows_of(w):
            if w < BLOCKS:
                return x_sb[:, w, :]
            return msg[:, (w - BLOCKS) // GROUP, (w - BLOCKS) % GROUP, 0:D]

        def sb(name, shape, dt):
            return ctx.enter_context(nc.sbuf_tensor(name, shape, dt))

        def ps(name, shape, dt=F32):
            return ctx.enter_context(nc.psum_tensor(name, shape, dt))

        def sem(name):
            return ctx.enter_context(nc.semaphore(name))

        x_sb = sb("x_sb", [P, BLOCKS, D], F32)
        stats = sb("stats", [P, ALL, 6], F32)
        mv = sb("mv", [P, ALL, 2], F32)
        var_eps = sb("var_eps", [P, ALL], F32)
        std = sb("std", [P, ALL], F32)
        rstd = sb("rstd", [P, ALL], F32)
        normed = sb("normed", [P, NBUF, D], F32)
        hT = sb("hT", [P, 2, P], F32)
        y_sb = sb("y_sb", [P, YBUF, RD], F32)
        w_sb = sb("w_sb", [P, R, D], F32)
        b_sb = sb("b_sb", [1, RD], F32)
        b_rest = y_sb[0:1, 0, :]
        b_part = sb("b_part", [1, 3, RD], BF16)
        b_split = sb("b_split", [3, RD], BF16)
        ones3 = sb("ones3", [3, P], BF16)
        ident = sb("ident", [P, P], F32)
        src_rows = sb("src_rows", [P, SLABS, P], I32)
        dst_rows = sb("dst_rows", [P, SLABS, P], I32)
        type_rows = sb("type_rows", [P, SLABS, P], I32)
        rel_rows = sb("rel_rows", [P, SLABS, P], F32)
        row_rows = rel_rows
        first_src = sb("first_src", [P, P], F32)
        first_type = sb("first_type", [P, P], F32)
        early_idx = sb("early_idx", [P, EARLY_TILES], I32)
        over = sb("over", [P, 2, EARLY_TILES], F32)
        of_rel = sb("of_rel", [P, R, EARLY_TILES], F32)
        idx_ring = sb("idx_ring", [P, RING, GROUP], I32)
        idx_tail = sb("idx_tail", [P, TAIL], I32)
        dstf_rows = type_rows[:, :, :].bitcast(F32)
        row_idx = src_rows[:, :, :].rearrange("p s e -> p (s e)")
        dst_col = dst_rows[:, :, :].rearrange("p s e -> p (s e)").bitcast(F32)
        tile_min = sb("tile_min", [P, SLABS], F32)
        tile_max = sb("tile_max", [P, SLABS], F32)
        NG = GROUPS + 1
        PER_SLAB = P // GROUP
        assert GROUPS == FULL_SLABS * PER_SLAB + REST_TILES // GROUP
        slab_ends = sb("slab_ends", [SLABS, 2, PER_SLAB + 1], F32)
        edge_ends = sb("edge_ends", [1, SLABS, 2, PER_SLAB + 1], F32)
        ends_int = sb("ends_int", [1, 2, NG], I32)
        win_ends = sb("win_ends", [1, 2, NG], I32)
        extras = sb("extras", [1, NG], F32)
        extras_upto = sb("extras_upto", [1, NG], F32)
        zeros1 = sb("zeros1", [1, NG], F32)
        plan = sb("plan", [1, NG, 3], I32)
        least_window = sb("least_window", [1, 1], F32)
        finish_early = sb("finish_early", [1, 1], I32)
        iota = sb("iota", [P, NPAD], F32)
        onehot = sb("onehot", [P, SETS, GROUP, P], F32)
        onehot_x = sb("onehot_x", [P, GROUP, P], F32)
        msg = sb("msg", [P, RING, GROUP, DA], F32)
        sums = sb("sums", [P, BLOCKS, DA], F32)
        deg = sb("deg", [P, BLOCKS], F32)
        rdeg = sb("rdeg", [P, BLOCKS], F32)

        ps_t = [ps(f"ps_t{i}", [P, P]) for i in range(2)]
        ps_y = [ps(f"ps_y{i}", [P, RD]) for i in range(2)]
        ps_e = [ps(f"ps_e{i}", [P, BANK_SLABS * P]) for i in range(2)]
        ps_first = [bank[:, 0:DA] for bank in (ps_e[0], ps_e[1], ps_y[0])]
        ps_x = ps("ps_x", [P, DA])

        x_landed = [sem(f"x_landed{c}") for c in range(CH)]
        pads_set = sem("pads_set")
        first_landed = sem("first_landed")
        first_made = sem("first_made")
        first_turned = sem("first_turned")
        early_idx_made = sem("early_idx_made")
        over_made = sem("over_made")
        of_rel_made = sem("of_rel_made")
        early_landed = [sem(f"early_landed{e}") for e in range(EARLY)]
        early_part = sem("early_part")
        early_added = sem("early_added")
        early_chosen = sem("early_chosen")
        iota_seeded = sem("iota_seeded")
        rows_landed = sem("rows_landed")
        dst_landed = sem("dst_landed")
        b_landed = sem("b_landed")
        w_landed = sem("w_landed")
        ident_made = sem("ident_made")
        iota_made = sem("iota_made")
        rows_made = sem("rows_made")
        rows_turned = sem("rows_turned")
        rows_copied = sem("rows_copied")
        b_steps = sem("b_steps")
        b_split_landed = sem("b_split_landed")
        ones3_set = sem("ones3_set")
        ends_made = sem("ends_made")
        stats_made = sem("stats_made")
        mv_made = sem("mv_made")
        var_made = sem("var_made")
        std_made = sem("std_made")
        rstd_made = sem("rstd_made")
        centred = sem("centred")
        turned = sem("turned")
        relu_made = sem("relu_made")
        projected = sem("projected")
        y_copied = sem("y_copied")
        y_stored = [sem(f"y_stored{i}") for i in range(YBUF)]
        edges_turned = sem("edges_turned")
        edges_copied = sem("edges_copied")
        ends_turned = sem("ends_turned")
        ends_reduced = sem("ends_reduced")
        ends_landed = sem("ends_landed")
        ends_clamped = sem("ends_clamped")
        plan_steps = sem("plan_steps")
        plan_made = sem("plan_made")
        ones_set = sem("ones_set")
        sums_zeroed = sem("sums_zeroed")
        gathered = [sem(f"gathered{i}") for i in range(RING)]
        tail_gathered = sem("tail_gathered")
        groups_begun = sem("groups_begun")
        idx_copied = sem("idx_copied")
        tail_copied = sem("tail_copied")
        slots_free = sem("slots_free")
        first_added = sem("first_added")
        extra_added = sem("extra_added")
        onehot_made = sem("onehot_made")
        first_summed = sem("first_summed")
        extra_made = sem("extra_made")
        extra_summed = sem("extra_summed")
        rdeg_made = sem("rdeg_made")
        mean_made = sem("mean_made")
        mean_scaled = sem("mean_scaled")
        result_made = sem("result_made")
        result_stored = sem("result_stored")

        block = ctx.enter_context(nc.Block())

        x_blocks = x[0:(BLOCKS - 1) * P, :].rearrange("(w p) f -> p w f", p=P)
        out_blocks = out[0:(BLOCKS - 1) * P, :].rearrange("(w p) f -> p w f", p=P)
        table_rows = table.rearrange("(g w p) f -> w p g f", g=R, p=P)
        PADS = 4

        def edge_loads(eng, sb_rows, dram, s0, twice, landed):
            eng.dma_start(sb_rows[:, s0:FULL_SLABS, :],
                          dram[s0 * P * P:FULL_SLABS * P * P].rearrange("(s p e) -> p s e", p=P, e=P)).then_inc(landed, 16)
            rest = FULL_SLABS * P * P
            eng.dma_start(sb_rows[0:REST_TILES, FULL_SLABS, :],
                          dram[rest:rest + REST_TILES * P].rearrange("(p e) -> p e", e=P)).then_inc(landed, 16)
            last = dram[E - LAST_EDGES:E].rearrange("(a e) -> a e", a=1)
            eng.dma_start(sb_rows[REST_TILES:REST_TILES + 1, FULL_SLABS, 0:LAST_EDGES], last).then_inc(landed, 16)
            if twice:
                eng.dma_start(sb_rows[REST_TILES:REST_TILES + 1, FULL_SLABS, LAST_EDGES:2 * LAST_EDGES],
                              last).then_inc(landed, 16)
        assert 2 * LAST_EDGES == P

        @block.sync
        def _(sp):
            for rows, dram in ((src_rows, src), (type_rows, edge_type)):
                sp.dma_start(rows[:, 0, :], dram[0:P * P].rearrange("(p e) -> p e", e=P)).then_inc(first_landed, 16)
            for c in range(CH):
                w0, w1 = CHUNKS[c]
                if c < CH - 1:
                    sp.dma_start(x_sb[:, w0:w1, :], x_blocks[:, w0:w1, :]).then_inc(x_landed[c], 16)
                else:
                    sp.dma_start(x_sb[:, w0:w1 - 1, :], x_blocks[:, w0:w1 - 1, :]).then_inc(x_landed[c], 16)
                    sp.dma_start(x_sb[0:LAST_ROWS, w1 - 1, :], x[N - LAST_ROWS:N, :]).then_inc(x_landed[c], 16)
                if c == 2:
                    sp.wait_ge(b_steps, 4)
                    sp.dma_start(b_split[:, :], b_part[:, :, :]).then_inc(b_split_landed, 16)
                    sp.wait_ge(pads_set, PADS)
                    edge_loads(sp, type_rows, edge_type, 1, False, rows_landed)
                    edge_loads(sp, src_rows, src, 1, False, rows_landed)
            for w in range(BLOCKS):
                sp.wait_ge(y_copied, w + 1)
                sp.dma_start(table_rows[w], y_sb[:, w % YBUF, :].rearrange("p (g f) -> p g f", g=R)).then_inc(
                    y_stored[w % YBUF], 16)
            sp.wait_ge(ends_reduced, 4)
            sp.dma_start(edge_ends[:, :, :, :], slab_ends[:, :, :]).then_inc(ends_landed, 16)
            for c in range(CH):
                sp.wait_ge(result_made, c + 1)
                w0, w1 = c * XCH, (c + 1) * XCH
                if c < CH - 1:
                    sp.dma_start(out_blocks[:, w0:w1, :], x_sb[:, w0:w1, :]).then_inc(result_stored, 16)
                else:
                    sp.dma_start(out_blocks[:, w0:w1 - 1, :], x_sb[:, w0:w1 - 1, :]).then_inc(result_stored, 16)
                    sp.dma_start(out[N - LAST_ROWS:N, :], x_sb[0:LAST_ROWS, w1 - 1, :]).then_inc(result_stored, 16)
            sp.wait_ge(result_stored, 16 * (CH + 1))

        @block.gpsimd
        def _(pool):
            pool.memset(ident[:, :], 0.0).then_inc(ident_made, 1)
            pool.wait_ge(ident_made, 1)
            pool.affine_select(out=ident[:, :], in_=ident[:, :], compare_op=ALU.not_equal, fill=1.0,
                               base=0, pattern=[[-1, P]], channel_multiplier=1).then_inc(ident_made, 1)
            pool.iota(iota[:, 0:XCH * P], [[1, XCH * P]], base=0, channel_multiplier=0,
                      allow_small_or_imprecise_dtypes=True).then_inc(iota_seeded, 1)
            pool.memset(x_sb[:, BLOCKS - 1, :], 0.0).then_inc(pads_set, 1)
            for rows in (src_rows, dst_rows, type_rows):
                pool.memset(rows[:, FULL_SLABS, :], 0).then_inc(pads_set, 1)
            pool.memset(msg[:, :, :, D:DA], 1.0).then_inc(ones_set, 1)
            pool.memset(sums[:, ZEROED_FIRST:ZEROED_NEXT, :], 0.0).then_inc(sums_zeroed, 1)

            pool.wait_ge(early_idx_made, 1)
            for t in range(EARLY_TILES):
                pool.indirect_dma_start(
                    rows_of(BLOCKS + t), None, x,
                    bass.IndirectOffsetOnAxis(ap=early_idx[:, t:t + 1], axis=0)).then_inc(early_landed[t // GROUP], 16)

            def gather(slot, j, rows, landed, idx):
                pool.indirect_dma_start(
                    msg[0:rows, slot, j, 0:D], None, table,
                    bass.IndirectOffsetOnAxis(ap=idx[0:rows, :], axis=0)).then_inc(landed, 16)

            for i in range(YBUF):
                pool.wait_ge(y_stored[i], 16 * len(range(i, BLOCKS, YBUF)))
            for s in range(EARLY, RING):
                pool.wait_ge(idx_copied, s - EARLY + 1)
                for j in range(GROUP):
                    gather(s, j, P, gathered[s], idx_ring[:, s, j:j + 1])
            with pool.Fori(1, GROUPS // RING) as r:
                for s in range(RING):
                    pool.wait_ge(idx_copied, r * RING + s + 1 - EARLY)
                    pool.wait_ge(slots_free, (r - 1) * RING + s + 1)
                    pool.sem_inc(groups_begun, 1)
                    for j in range(GROUP):
                        gather(s, j, P, gathered[s], idx_ring[:, s, j:j + 1])
            pool.wait_ge(tail_copied, 1)
            pool.wait_ge(slots_free, GROUPS - RING + 1)
            for j in range(TAIL):
                gather(0, j, P if j < TAIL - 1 else LAST_EDGES, tail_gathered, idx_tail[:, j:j + 1])

        @block.scalar
        def _(act):
            act.dma_start(b_sb[:, :], b.rearrange("(a g) f -> a (g f)", a=1)).then_inc(b_landed, 16)
            act.dma_start(w_sb[:, :, :], W.rearrange("g k f -> k g f")).then_inc(w_landed, 16)

            def root(c):
                w0, w1 = CHUNKS[c]
                act.wait_ge(var_made, c + 1)
                act.activation(std[:, w0:w1], var_eps[:, w0:w1], ACT.Sqrt).then_inc(std_made, 1)

            def copy_turned(k, to, turned_sem, copied_sem):
                if 0 <= k < BANKS:
                    k0 = k * BANK_SLABS * P
                    n = min(BANK_SLABS * P, SLABS * P - k0)
                    act.wait_ge(turned_sem, k + 1)
                    act.activation(to[:, k0:k0 + n], ps_e[k % 2][:, 0:n], ACT.Copy).then_inc(copied_sem, 1)

            act.wait_ge(iota_seeded, 1)
            for c in range(1, CH):
                act.activation(iota[:, c * XCH * P:(c + 1) * XCH * P], iota[:, 0:XCH * P], ACT.Copy,
                               bias=float(c * XCH * P)).then_inc(iota_made, 1)
            act.wait_ge(pads_set, PADS)
            edge_loads(act, dst_rows, dst, 0, True, dst_landed)
            root(0)
            for w in range(ALL + 1):
                for c, (w0, w1) in enumerate(CHUNKS[:-1]):
                    if w == (XCH // 2 if c == 0 else w0 - ROOT_LEAD if c < CH else w1 - 2):
                        root(c + 1)
                if w < ALL:
                    act.wait_ge(turned, w + 1)
                    if w >= 2:
                        act.wait_ge(projected, w - 1)
                    act.activation(hT[:, w % 2, :], ps_t[w % 2][:, :], ACT.Relu).then_inc(relu_made, 1)
                v = w - 1
                if v >= 0:
                    act.wait_ge(projected, v + 1)
                if 0 <= v < BLOCKS:
                    if v >= YBUF:
                        act.wait_ge(y_stored[v % YBUF], 16 * (v // YBUF))
                    act.activation(y_sb[:, v % YBUF, :], ps_y[v % 2][:, :], ACT.Copy).then_inc(y_copied, 1)
                if v >= BLOCKS:
                    act.wait_ge(of_rel_made, R)
                    act.activation(rows_of(v), ps_y[v % 2][:, 0:D], ACT.Copy,
                                   scale=of_rel[:, 0, v - BLOCKS:v - BLOCKS + 1]).then_inc(early_part, 1)
                copy_turned(w - ROWS_AT, row_idx, rows_turned, rows_copied)
                copy_turned(w - DST_AT, dst_col, edges_turned, edges_copied)
                if w == BLOCKS - 1:
                    act.wait_ge(rows_copied, BANKS)
                    for g in range(EARLY, RING + EARLY):
                        act.activation(idx_ring[:, g % RING, :], row_idx[:, g * GROUP:(g + 1) * GROUP],
                                       ACT.Copy).then_inc(idx_copied, 1)
                    act.activation(idx_tail[:, :], row_idx[:, GROUPS * GROUP:TILES], ACT.Copy).then_inc(tail_copied, 1)

            def later_indices(g, slot):
                act.wait_ge(slots_free, g - RING + 1)
                act.activation(idx_ring[:, slot, :], row_idx[:, bass.ds(g * GROUP, GROUP)],
                               ACT.Copy).then_inc(idx_copied, 1)

            with act.Fori(1, GROUPS // RING - 1) as r:
                for s in range(RING):
                    later_indices(r * RING + EARLY + s, (EARLY + s) % RING)
            for g in range(GROUPS - RING + EARLY, GROUPS):
                later_indices(g, g % RING)
            for c in range(CH):
                act.wait_ge(rdeg_made, 2 if c < CH - 1 else 4)
                for w in range(c * XCH + DVE_SHARE, (c + 1) * XCH):
                    last = act.activation(sums[:, w, 0:D], sums[:, w, 0:D], ACT.Relu, scale=rdeg[:, w:w + 1])
                last.then_inc(mean_made, 1)

        @block.tensor
        def _(pe):
            pe.wait_ge(ident_made, 2)

            def turn(k, rows, turned_sem, copied_sem):
                if 0 <= k < BANKS:
                    if k >= 2:
                        pe.wait_ge(copied_sem, k - 1)
                    for i in range(min(BANK_SLABS, SLABS - k * BANK_SLABS)):
                        last = pe.transpose(ps_e[k % 2][:, i * P:(i + 1) * P], rows[:, k * BANK_SLABS + i, :], ident[:, :])
                    last.then_inc(turned_sem, 1)

            def turn_ends():
                pe.wait_ge(rows_copied, BANKS)
                for m, ends in enumerate((tile_min, tile_max)):
                    pe.transpose(ps_e[m][0:SLABS, 0:P], ends[:, :], ident[:, :]).then_inc(ends_turned, 1)

            pe.wait_ge(first_made, 2)
            for i, rows in enumerate((first_src, first_type)):
                pe.transpose(ps_e[i][:, 0:P], rows[:, :], ident[:, :]).then_inc(first_turned, 1)

            def sum_tiles(to, onehots, slot, tiles, last_rows):
                for j in range(tiles):
                    rows = P if j < tiles - 1 else last_rows
                    last = pe.matmul(to, onehots[0:rows, j, :], msg[0:rows, slot, j, :],
                                     start=(j == 0), stop=(j == tiles - 1))
                return last

            def sum_windows(g, slot, landed, level, tiles, last_rows):
                pe.wait_ge(onehot_made, g + 1)
                pe.wait_ge(landed, level)
                sum_tiles(ps_first[set_of(slot)], onehot[:, set_of(slot), :, :], slot, tiles, last_rows).then_inc(
                    first_summed, 1)
                count = pe.value_load(plan[0:1, bass.ds(g, 1), 1:2], min_val=1, max_val=BLOCKS)
                with pe.If(count > 1):
                    before = pe.value_load(plan[0:1, bass.ds(g, 1), 2:3], min_val=0, max_val=NG * BLOCKS)
                    with pe.Fori(1, count) as i:
                        pe.wait_ge(extra_made, before + i)
                        sum_tiles(ps_x[:, :], onehot_x, slot, tiles, last_rows).then_inc(extra_summed, 1)

            def sum_early(s):
                if s == 0:
                    pe.wait_ge(plan_made, 1)
                    pe.wait_ge(ones_set, 1)
                    pe.wait_ge(edges_copied, BANKS)
                sum_windows(s, s, early_chosen, (s + 1) * GROUP, GROUP, P)

            pe.wait_ge(w_landed, 16)
            for w in range(ALL + 1):
                if w < ALL:
                    pe.wait_ge(centred, w + 1)
                    if w >= 2:
                        pe.wait_ge(relu_made, w - 1)
                    pe.transpose(ps_t[w % 2][:, :], normed[:, w % NBUF, :], ident[:, :]).then_inc(turned, 1)
                if w >= 1:
                    v = w - 1
                    if v == 0:
                        pe.wait_ge(b_split_landed, 16)
                        pe.wait_ge(ones3_set, 1)
                    if 2 <= v < BLOCKS + 2:
                        pe.wait_ge(y_copied, v - 1)
                    if v >= BLOCKS + 2:
                        pe.wait_ge(early_chosen, v - 1 - BLOCKS)
                    pe.matmul(ps_y[v % 2][:, :], ones3[:, :], b_split[:, :], start=True, stop=False)
                    pe.wait_ge(relu_made, v + 1)
                    pe.matmul(ps_y[v % 2][:, :], hT[:, v % 2, :], w_sb[:, :, :].rearrange("k g f -> k (g f)"),
                              start=False, stop=True).then_inc(projected, 1)
                if w == ROWS_AT:
                    pe.wait_ge(early_idx_made, 1)
                    pe.wait_ge(over_made, 2)
                    pe.wait_ge(rows_made, 3)
                turn(w - ROWS_AT, row_rows, rows_turned, rows_copied)
                if w == ENDS_AT:
                    pe.wait_ge(ends_made, 3)
                    turn_ends()
                if w == DST_AT:
                    pe.wait_ge(ends_reduced, 4)
                turn(w - DST_AT, dstf_rows, edges_turned, edges_copied)
                e, j = divmod(w - BLOCKS - SUM_AT, GROUP)
                if j == 0 and 1 <= e < EARLY:
                    sum_early(e - 1)

            sum_early(EARLY - 1)
            for s in range(EARLY, RING):
                sum_windows(s, s, gathered[s], 16 * GROUP, GROUP, P)
            with pe.Fori(1, GROUPS // RING) as r:
                for s in range(RING):
                    sum_windows(r * RING + s, s, gathered[s], (r if s < EARLY else r + 1) * (16 * GROUP), GROUP, P)
            sum_windows(GROUPS, 0, tail_gathered, 16 * TAIL, TAIL, LAST_EDGES)

        @block.vector
        def _(dve):
            dve.memset(sums[:, 0:ZEROED_FIRST, :], 0.0).then_inc(sums_zeroed, 1)
            dve.wait_ge(first_landed, 32)
            dve.tensor_copy(first_src[:, :], src_rows[:, 0, :]).then_inc(first_made, 1)
            dve.tensor_copy(first_type[:, :], type_rows[:, 0, :]).then_inc(first_made, 1)
            dve.wait_ge(first_turned, 1)
            dve.tensor_copy(early_idx[:, :], ps_e[0][:, 0:EARLY_TILES]).then_inc(early_idx_made, 1)
            dve.wait_ge(first_turned, 2)
            for i in range(2):
                dve.tensor_scalar(over[:, i, :], ps_e[1][:, 0:EARLY_TILES], float((i + 1) * REL_EDGE), None,
                                  ALU.is_ge).then_inc(over_made, 1)
            dve.wait_ge(over_made, 2)
            dve.tensor_scalar(of_rel[:, 0, :], over[:, 0, :], -1.0, 1.0, ALU.mult, ALU.add).then_inc(of_rel_made, 1)
            dve.tensor_tensor(of_rel[:, 1, :], over[:, 0, :], over[:, 1, :], ALU.subtract).then_inc(of_rel_made, 1)
            dve.tensor_copy(of_rel[:, 2, :], over[:, 1, :]).then_inc(of_rel_made, 1)
            dve.memset(ones3[:, :], 1.0).then_inc(ones3_set, 1)

            def bias_parts():
                dve.wait_ge(b_landed, 16)
                dve.tensor_copy(b_part[:, 0, :], b_sb[:, :]).then_inc(b_steps, 1)
                dve.wait_ge(b_steps, 1)
                dve.tensor_tensor(b_rest, b_sb[:, :], b_part[:, 0, :], ALU.subtract).then_inc(b_steps, 1)
                dve.wait_ge(b_steps, 2)
                dve.tensor_copy(b_part[:, 1, :], b_rest).then_inc(b_steps, 1)
                dve.wait_ge(b_steps, 3)
                dve.tensor_tensor(b_part[:, 2, :], b_rest, b_part[:, 1, :], ALU.subtract).then_inc(b_steps, 1)

            def row_stats(w):
                dve.bn_stats(stats[:, w, :], rows_of(w)).then_inc(stats_made, 1)

            def variances(c):
                w0, w1 = CHUNKS[c]
                dve.wait_ge(stats_made, w1)
                for w in range(w0, w1):
                    dve.bn_aggr(mv[:, w, :], stats[:, w, :]).then_inc(mv_made, 1)
                dve.wait_ge(mv_made, w1)
                dve.tensor_scalar(var_eps[:, w0:w1], mv[:, w0:w1, 1], EPS, None, ALU.add).then_inc(var_made, 1)

            def rows_arrived(c):
                if c < CH:
                    dve.wait_ge(x_landed[c], 16 if c < CH - 1 else 32)
                else:
                    dve.wait_ge(early_landed[c - CH], 16 * GROUP)

            def norm_stats(c):
                rows_arrived(c)
                for w in range(*CHUNKS[c]):
                    row_stats(w)
                variances(c)

            def roots(c):
                w0, w1 = CHUNKS[c]
                dve.wait_ge(std_made, c + 1)
                dve.reciprocal(rstd[:, w0:w1], std[:, w0:w1]).then_inc(rstd_made, 1)
                dve.wait_ge(rstd_made, c + 1)

            def norm_rows(w):
                if w >= NBUF:
                    dve.wait_ge(turned, w - NBUF + 1)
                dve.tensor_scalar(normed[:, w % NBUF, :], rows_of(w), mv[:, w, 0:1], rstd[:, w:w + 1],
                                  ALU.subtract, ALU.mult).then_inc(centred, 1)

            def norm(c):
                roots(c)
                for w in range(*CHUNKS[c]):
                    norm_rows(w)

            def choose(t, g):
                v = BLOCKS + t
                if g == 1:
                    dve.wait_ge(early_part, t + 1)
                else:
                    dve.wait_ge(early_added, (R - 2) * t + g - 1)
                dve.scalar_tensor_tensor(
                    out=rows_of(v), in0=ps_y[v % 2][:, g * D:(g + 1) * D], scalar=of_rel[:, g, t:t + 1],
                    in1=rows_of(v), op0=ALU.mult, op1=ALU.add).then_inc(early_added if g < R - 1 else early_chosen, 1)

            def edge_rows(step):
                if step == 0:
                    dve.wait_ge(rows_landed, 16 * 6)
                    dve.tensor_scalar(rel_rows[:, :, :], type_rows[:, :, :], float(2 * REL_EDGE), None,
                                      ALU.is_ge).then_inc(rows_made, 1)
                if step == 1:
                    dve.wait_ge(rows_made, 1)
                    dve.scalar_tensor_tensor(out=rel_rows[:, :, :], in0=type_rows[:, :, :], scalar=float(REL_EDGE),
                                             in1=rel_rows[:, :, :], op0=ALU.is_ge, op1=ALU.add).then_inc(rows_made, 1)
                if step == 2:
                    dve.wait_ge(rows_made, 2)
                    dve.scalar_tensor_tensor(out=row_rows[:, :, :], in0=rel_rows[:, :, :], scalar=float(NPAD),
                                             in1=src_rows[:, :, :], op0=ALU.mult, op1=ALU.add).then_inc(rows_made, 1)

            def tile_ends(step):
                if step == 0:
                    dve.wait_ge(dst_landed, 16 * 4)
                    dve.tensor_copy(dstf_rows[:, :, :], dst_rows[:, :, :]).then_inc(ends_made, 1)
                    dve.wait_ge(ends_made, 1)
                    dve.tensor_reduce(tile_min[:, :], dstf_rows[:, :, :], AX_X, ALU.min).then_inc(ends_made, 1)
                if step == 1:
                    dve.tensor_reduce(tile_max[:, :], dstf_rows[:, :, :], AX_X, ALU.max).then_inc(ends_made, 1)

            def group_ends():
                for m, op in enumerate((ALU.min, ALU.max)):
                    dve.wait_ge(ends_turned, m + 1)
                    turned_ends = ps_e[m][0:SLABS, 0:P]
                    dve.tensor_reduce(slab_ends[:, m, 0:PER_SLAB], turned_ends.rearrange("s (g j) -> s g j", j=GROUP),
                                      AX_X, op).then_inc(ends_reduced, 1)
                    t0 = REST_TILES + 1 - TAIL
                    dve.tensor_reduce(slab_ends[:, m, PER_SLAB:PER_SLAB + 1], turned_ends[:, t0:t0 + TAIL],
                                      AX_X, op).then_inc(ends_reduced, 1)

            plan_count = [0]

            def step(ins):
                plan_count[0] += 1
                ins.then_inc(plan_steps, 1)
                dve.wait_ge(plan_steps, plan_count[0])

            def make_plan():
                dve.wait_ge(ends_landed, 16)
                full = FULL_SLABS * PER_SLAB
                for g0, g1, ends in (
                        (0, full, edge_ends[:, 0:FULL_SLABS, :, 0:PER_SLAB].rearrange("a s m j -> a m s j")),
                        (full, GROUPS, edge_ends[:, FULL_SLABS, :, 0:GROUPS - full]),
                        (GROUPS, NG, edge_ends[:, FULL_SLABS, :, PER_SLAB:PER_SLAB + 1])):
                    to = ends_int[:, :, g0:g1]
                    if g0 == 0:
                        to = to.rearrange("a m (s j) -> a m s j", j=PER_SLAB)
                    dve.tensor_scalar(to, ends, 0.0, float(N - 1), ALU.max, ALU.min).then_inc(ends_clamped, 1)
                dve.wait_ge(ends_clamped, 3)
                step(dve.tensor_scalar(win_ends[:, :, :], ends_int[:, :, :], P.bit_length() - 1, None,
                                       ALU.logical_shift_right))
                step(dve.tensor_tensor(extras[:, :], win_ends[:, 1, :], win_ends[:, 0, :], ALU.subtract))
                step(dve.memset(zeros1[:, :], 0.0))
                step(dve.tensor_tensor_scan(extras_upto[:, :], extras[:, :], zeros1[:, :], 0.0, ALU.add, ALU.add))
                step(dve.tensor_copy(plan[:, :, 0], win_ends[:, 0, :]))
                step(dve.tensor_scalar(plan[:, :, 1], extras[:, :], 1.0, None, ALU.add))
                step(dve.tensor_tensor(plan[:, :, 2], extras_upto[:, :], extras[:, :], ALU.subtract))
                step(dve.tensor_reduce(least_window[:, :], win_ends[:, 0, FINISH_FROM:NG], AX_X, ALU.min))
                step(dve.tensor_scalar(finish_early[:, :], least_window[:, :], float(FINISH_BLOCKS), None, ALU.is_ge))
                dve.sem_inc(plan_made, 1)

            def load_first(g):
                return dve.value_load(plan[0:1, bass.ds(g, 1), 0:1], min_val=0, max_val=BLOCKS - 1)

            def one_hots(to, g, w, made):
                dve.tensor_tensor(
                    to, dst_col[:, bass.ds(g * GROUP, GROUP)].unsqueeze(2).to_broadcast([P, GROUP, P]),
                    iota[:, bass.ds(w * P, P)].unsqueeze(1).to_broadcast([P, GROUP, P]),
                    ALU.is_equal).then_inc(made, 1)

            def add(bank, w, added):
                where = sums[:, bass.ds(w, 1), :].rearrange("p a f -> p (a f)")
                dve.tensor_tensor(where, where, bank, ALU.add).then_inc(added, 1)

            def add_windows(g, slot, first=None):
                first = load_first(g) if first is None else first
                count = dve.value_load(plan[0:1, bass.ds(g, 1), 1:2], min_val=1, max_val=BLOCKS)
                dve.wait_ge(first_summed, g + 1)
                add(ps_first[set_of(slot)], first, first_added)
                with dve.If(count > 1):
                    before = dve.value_load(plan[0:1, bass.ds(g, 1), 2:3], min_val=0, max_val=NG * BLOCKS)
                    with dve.Fori(1, count) as i:
                        w = nc.s_assert_within(first + i, 0, BLOCKS - 1, skip_runtime_bounds_check_because=
                                               "the plan's windows end at the last one: the dst behind it are clamped")
                        one_hots(onehot_x[:, :, :], g, w, extra_made)
                        dve.wait_ge(extra_summed, before + i)
                        dve.wait_ge(first_added, g + 1)
                        add(ps_x[:, :], w, extra_added)
                        dve.wait_ge(extra_added, before + i)

            def free_slot(g):
                dve.wait_ge(first_added, g + 1)
                dve.sem_inc(slots_free, 1)

            def ring_step(g, s):
                one_hots(onehot[:, set_of(s + 1), :, :], g + 1, load_first(g + 1), onehot_made)
                add_windows(g, s)
                free_slot(g)

            def divide(c0, c1, steps):
                b0, b1 = c0 * XCH, c1 * XCH
                dve.tensor_scalar(deg[:, b0:b1], sums[:, b0:b1, D], 1.0, None, ALU.max).then_inc(rdeg_made, 1)
                dve.wait_ge(rdeg_made, steps + 1)
                dve.reciprocal(rdeg[:, b0:b1], deg[:, b0:b1]).then_inc(rdeg_made, 1)
                dve.wait_ge(rdeg_made, steps + 2)
                for c in range(c0, c1):
                    w0, w1 = c * XCH, (c + 1) * XCH
                    for w in range(w0, w0 + DVE_SHARE):
                        dve.tensor_scalar(sums[:, w, 0:D], sums[:, w, 0:D], rdeg[:, w:w + 1], 0.0,
                                          ALU.mult, ALU.max).then_inc(mean_scaled, 1)
                    dve.wait_ge(mean_scaled, (c + 1) * DVE_SHARE)
                    dve.wait_ge(mean_made, c + 1)
                    dve.tensor_tensor(x_sb[:, w0:w1, :], sums[:, w0:w1, 0:D],
                                      x_sb[:, w0:w1, :], ALU.add).then_inc(result_made, 1)

            bias_parts()
            norm_stats(0)
            for c in range(CH):
                if c == 2:
                    dve.memset(sums[:, ZEROED_NEXT:BLOCKS, :], 0.0).then_inc(sums_zeroed, 1)
                if c > 0:
                    norm_stats(c + 1)
                norm(c)
                if c == 0:
                    norm_stats(1)
                if 1 <= c < 4:
                    edge_rows(c - 1)
                if 4 <= c < 6:
                    tile_ends(c - 4)
                if c == CH - 1:
                    group_ends()
            for c in range(CH, CH + EARLY):
                s = c - CH - 1
                roots(c)
                if c + 1 < CH + EARLY:
                    rows_arrived(c + 1)
                for j, w in enumerate(range(*CHUNKS[c])):
                    t = w - BLOCKS - LAG
                    if t >= 0:
                        for g in range(1, R - 1):
                            choose(t, g)
                    norm_rows(w)
                    if t >= 0:
                        choose(t, R - 1)
                    if s >= 0 and j == ONEHOT_AT:
                        first = load_first(s)
                        one_hots(onehot[:, set_of(s), :, :], s, first, onehot_made)
                    if c + 1 < CH + EARLY:
                        if j < GROUP // 2:
                            row_stats(CHUNKS[c + 1][0] + 2 * j)
                            row_stats(CHUNKS[c + 1][0] + 2 * j + 1)
                        if j == GROUP // 2:
                            variances(c + 1)
                    if j == SUM_AT - 1 + LAG:
                        if s < 0:
                            make_plan()
                            dve.wait_ge(edges_copied, BANKS)
                            dve.wait_ge(iota_made, CH - 1)
                            dve.wait_ge(sums_zeroed, 3)
                        else:
                            add_windows(s, s, first)
                            free_slot(s)
            for t in range(EARLY_TILES - LAG, EARLY_TILES):
                for g in range(1, R):
                    choose(t, g)
            one_hots(onehot[:, set_of(EARLY - 1), :, :], EARLY - 1, load_first(EARLY - 1), onehot_made)
            for s in range(EARLY - 1, RING):
                ring_step(s, s)
            with dve.Fori(1, GROUPS // RING - 1) as r:
                for s in range(RING):
                    ring_step(r * RING + s, s)
            early = dve.value_load(finish_early[0:1, 0:1], min_val=0, max_val=1)
            with dve.If(early > 0):
                divide(0, CH - 1, 0)
            with dve.Fori(GROUPS // RING - 1, GROUPS // RING) as r:
                for s in range(RING):
                    ring_step(r * RING + s, s)
            add_windows(GROUPS, 0)
            dve.wait_ge(first_added, NG)
            with dve.If(early < 1):
                divide(0, CH - 1, 0)
            divide(CH - 1, CH, 2)


_INS = ['x', 'src', 'dst', 'edge_type_30', 'L0_gnn_W', 'L0_gnn_b']
_OUTS = [((6250, 128), 'float32')]


def kernel(**inputs):
    import numpy as _np
    import concourse.bacc as _bacc
    from concourse import mybir as _mybir
    from concourse.bass_utils import run_bass_kernel_spmd as _run

    nc = _bacc.Bacc("TRN2", target_bir_lowering=False, num_devices=1)
    arrays, args = {}, []
    for name in _INS:
        a = _np.ascontiguousarray(inputs[name])
        arrays[f"in_{name}_dram"] = a
        args.append(nc.dram_tensor(f"in_{name}_dram", a.shape, _mybir.dt.from_np(a.dtype), kind="ExternalInput").ap())
    for i, (shape, dtype) in enumerate(_OUTS):
        dt = _mybir.dt.from_np(_np.dtype(dtype))
        args.append(nc.dram_tensor(f"out_{i}_dram", shape, dt, kind="ExternalOutput").ap())
    bass_gnn_mean_aggregate_kernel(nc, *args)
    r = _run(nc, [arrays], core_ids=[0])
    got = tuple(r.results[0][f"out_{i}_dram"] for i in range(len(_OUTS)))
    return got[0]
```
